# Optimizing a Trainium2 kernel written in Bass

```python
import numpy as np
import jax
import jax.numpy as jnp

def _softmax(x, axis=-1):
    return jax.nn.softmax(x, axis=axis)

def _gelu(x):
    return jax.nn.gelu(x, approximate=True)

def _silu(x):
    return jax.nn.silu(x)

def _sigmoid(x):
    return jax.nn.sigmoid(x)

def _layernorm(x, axis=-1, eps=1e-05):
    m = jnp.mean(x, axis=axis, keepdims=True)
    v = jnp.var(x, axis=axis, keepdims=True)
    return (x - m) / jnp.sqrt(v + eps)

def _scatter_add(tgt, idx, src, axis=0):
    return tgt.at[idx].add(src)

def _segment_sum(src, seg, n):
    return jax.ops.segment_sum(src, seg, n)
kernel_name = 'mk_metaformer_d2_conv_nhwc256_r4_7118b2'

def setup_inputs(seed: int=0):
    np.random.seed(seed)
    _w = jnp.asarray

    def _rec_inputs():
        import jax
        import jax.numpy as jnp
        _gk = jax.random.key(seed)
        x = -0.0002023 + 1 * jax.random.normal(jax.random.fold_in(_gk, 1), (8, 56, 56, 64), jnp.float32)
        return x
    x = _rec_inputs()

    def _L0_conv_setup():
        import jax, jax.numpy as jnp
        import numpy as np
        NH, NWIN, TOPK = (8, 7, 4)
        key = jax.random.key(seed)
        ks = jax.random.split(key, 7)
        B, H, W, C = (8, 56, 56, 64)
        return {'x': jax.random.normal(ks[0], (B, H, W, C), jnp.float32), 'qkv_w': jax.random.normal(ks[1], (3 * C, C), jnp.float32) * C ** (-0.5), 'qkv_b': jax.random.normal(ks[2], (3 * C,), jnp.float32) * 0.02, 'lepe_w': jax.random.normal(ks[3], (C, 1, 3, 3), jnp.float32) * 0.1, 'lepe_b': jax.random.normal(ks[4], (C,), jnp.float32) * 0.02, 'out_w': jax.random.normal(ks[5], (C, C), jnp.float32) * C ** (-0.5), 'out_b': jax.random.normal(ks[6], (C,), jnp.float32) * 0.02}
    _L0_conv_all = _L0_conv_setup()
    _L0_conv_in = {k: v for k, v in _L0_conv_all.items() if k in ('qkv_w', 'qkv_b', 'lepe_w', 'lepe_b', 'out_w', 'out_b')}
    del _L0_conv_all

    def _L0_ffn_setup():
        import jax, jax.numpy as jnp
        import numpy as np
        NUM_EXPERTS = 8
        TOP_K = 2
        B, S, D = (8, 2048, 64)

        def _moe(tokens, router_w, w1, b1, w2, b2):
            N = tokens.shape[0]
            E = router_w.shape[0]
            logits = tokens.astype(jnp.float32) @ router_w.astype(jnp.float32).T
            probs = jax.nn.softmax(logits, axis=-1)
            rw, re = jax.lax.top_k(probs, TOP_K)
            if TOP_K > 1:
                rw = rw / jnp.maximum(rw.sum(-1, keepdims=True), 1e-12)
            rw = rw.astype(tokens.dtype)
            combine = jnp.zeros((N, E), tokens.dtype).at[jnp.arange(N)[:, None], re].set(rw)
            out = tokens
            for e in range(E):
                h = jax.nn.gelu(tokens @ w1[e] + b1[e], approximate=False)
                y = h @ w2[e] + b2[e]
                out = out + combine[:, e:e + 1] * y
            return out
        key = jax.random.key(seed)
        ks = jax.random.split(key, 4)
        scale = 1.0 / np.sqrt(D).astype(np.float32)
        return {'input_embeddings': jax.random.normal(ks[0], (B, S, D), jnp.float32), 'router_w': jax.random.normal(ks[1], (NUM_EXPERTS, D), jnp.float32) * scale, 'w1': jax.random.normal(ks[2], (NUM_EXPERTS, D, D), jnp.float32) * scale, 'b1': jnp.zeros((NUM_EXPERTS, D), jnp.float32), 'w2': jax.random.normal(ks[3], (NUM_EXPERTS, D, D), jnp.float32) * scale, 'b2': jnp.zeros((NUM_EXPERTS, D), jnp.float32)}
    _L0_ffn_all = _L0_ffn_setup()
    _L0_ffn_in = {k: v for k, v in _L0_ffn_all.items() if k in ('router_w', 'w1', 'b1', 'w2', 'b2')}
    del _L0_ffn_all

    def _L1_conv_setup():
        import jax, jax.numpy as jnp
        import numpy as np
        H_CONST = 1.0

        def binarize(w, H=H_CONST):
            return jnp.where(w >= 0, H, -H).astype(w.dtype)
        key = jax.random.key(seed)
        k1, k2 = jax.random.split(key)
        x = jax.random.normal(k1, (32, 56, 56, 64), dtype=jnp.float32)
        kernel = jax.random.normal(k2, (3, 3, 64, 64), dtype=jnp.float32) * 0.05
        return {'x': x, 'kernel': kernel}
    _L1_conv_all = _L1_conv_setup()
    _L1_conv_in = {k: v for k, v in _L1_conv_all.items() if k in ('kernel',)}
    del _L1_conv_all

    def _L1_ffn_setup():
        import jax, jax.numpy as jnp
        import numpy as np
        B, T, D, H, E = (16, 1024, 64, 128, 8)
        key = jax.random.key(seed)
        ks = jax.random.split(key, 5)
        x = jax.random.normal(ks[0], (B, T, D), dtype=jnp.float32)
        gate_w = jax.random.normal(ks[1], (D, E), dtype=jnp.float32) * 0.02
        gate_b = jnp.zeros((E,), dtype=jnp.float32)
        W1 = jax.random.normal(ks[2], (E, D, H), dtype=jnp.float32) * 0.02
        b1 = jnp.zeros((E, H), dtype=jnp.float32)
        W2 = jax.random.normal(ks[3], (E, H, D), dtype=jnp.float32) * 0.02
        b2 = jnp.zeros((E, D), dtype=jnp.float32)
        return {'x': x, 'gate_w': gate_w, 'gate_b': gate_b, 'W1': W1, 'b1': b1, 'W2': W2, 'b2': b2}
    _L1_ffn_all = _L1_ffn_setup()
    _L1_ffn_in = {k: v for k, v in _L1_ffn_all.items() if k in ('gate_w', 'gate_b', 'W1', 'b1', 'W2', 'b2')}
    del _L1_ffn_all
    return {'x': x, 'L0_conv_qkv_w': _L0_conv_in['qkv_w'], 'L0_conv_qkv_b': _L0_conv_in['qkv_b'], 'L0_conv_lepe_w': _L0_conv_in['lepe_w'], 'L0_conv_lepe_b': _L0_conv_in['lepe_b'], 'L0_conv_out_w': _L0_conv_in['out_w'], 'L0_conv_out_b': _L0_conv_in['out_b'], 'L0_ffn_router_w': _L0_ffn_in['router_w'], 'L0_ffn_w1': _L0_ffn_in['w1'], 'L0_ffn_b1': _L0_ffn_in['b1'], 'L0_ffn_w2': _L0_ffn_in['w2'], 'L0_ffn_b2': _L0_ffn_in['b2'], 'L1_conv_kernel': _L1_conv_in['kernel'], 'L1_ffn_gate_w': _L1_ffn_in['gate_w'], 'L1_ffn_gate_b': _L1_ffn_in['gate_b'], 'L1_ffn_W1': _L1_ffn_in['W1'], 'L1_ffn_b1': _L1_ffn_in['b1'], 'L1_ffn_W2': _L1_ffn_in['W2'], 'L1_ffn_b2': _L1_ffn_in['b2']}

def reference(x, L0_conv_qkv_w, L0_conv_qkv_b, L0_conv_lepe_w, L0_conv_lepe_b, L0_conv_out_w, L0_conv_out_b, L0_ffn_router_w, L0_ffn_w1, L0_ffn_b1, L0_ffn_w2, L0_ffn_b2, L1_conv_kernel, L1_ffn_gate_w, L1_ffn_gate_b, L1_ffn_W1, L1_ffn_b1, L1_ffn_W2, L1_ffn_b2):
    import jax
    import jax.numpy as jnp

    def _L0_conv_ref(x, qkv_w, qkv_b, lepe_w, lepe_b, out_w, out_b):
        import jax, jax.numpy as jnp
        import numpy as np
        NH, NWIN, TOPK = (8, 7, 4)
        B, H, W, C = x.shape
        nh, nwin, topk = (NH, NWIN, TOPK)
        hd = C // nh
        rh, rw = (H // nwin, W // nwin)
        nreg, S = (nwin * nwin, rh * rw)
        scale = C ** (-0.5)
        xc = jnp.transpose(x, (0, 3, 1, 2))
        qkv = jnp.einsum('bchw,oc->bohw', xc, qkv_w) + qkv_b[None, :, None, None]
        q, k, v = jnp.split(qkv, 3, axis=1)

        def pool(t):
            t = t.reshape(B, C, nwin, rh, nwin, rw)
            return t.mean(axis=(3, 5))
        q_r = jax.lax.stop_gradient(pool(q)).transpose(0, 2, 3, 1).reshape(B, nreg, C)
        k_r = jax.lax.stop_gradient(pool(k)).reshape(B, C, nreg)
        a_r = q_r @ k_r
        idx_r = jax.lax.top_k(a_r, topk)[1]

        def g2s(t):
            t = t.reshape(B, nh, hd, nwin, rh, nwin, rw)
            return jnp.einsum('bmdhpwq->bmhwpqd', t).reshape(B, nh, nreg, S, hd)
        qs, ks_, vs = (g2s(q), g2s(k), g2s(v))
        rg = jnp.broadcast_to(idx_r[:, None], (B, nh, nreg, topk))
        bI = jnp.arange(B)[:, None, None, None]
        hI = jnp.arange(nh)[None, :, None, None]
        key_g = ks_[bI, hI, rg]
        val_g = vs[bI, hI, rg]
        TS = topk * S
        attn = jnp.einsum('bhnsd,bhnkd->bhnsk', qs * scale, key_g.reshape(B, nh, nreg, TS, hd))
        k2 = TS // 8
        score, index = jax.lax.top_k(attn, k2)
        vflat = val_g.reshape(B, nh, nreg, TS, hd)
        bI2 = jnp.arange(B)[:, None, None, None, None]
        hI2 = jnp.arange(nh)[None, :, None, None, None]
        nI2 = jnp.arange(nreg)[None, None, :, None, None]
        v_sel = vflat[bI2, hI2, nI2, index]
        a_g = jax.nn.softmax(score, axis=-1)
        out = jnp.einsum('bhnsk,bhnskd->bhnsd', a_g, v_sel)
        out = out.reshape(B, nh, nwin, nwin, rh, rw, hd)
        out = jnp.einsum('bmhwpqd->bmdhpwq', out).reshape(B, C, H, W)
        lepe = jax.lax.conv_general_dilated(v, lepe_w, (1, 1), 'SAME', feature_group_count=C) + lepe_b[None, :, None, None]
        out = out + lepe
        out = jnp.einsum('bchw,oc->bohw', out, out_w) + out_b[None, :, None, None]
        return jnp.transpose(out, (0, 2, 3, 1))

    def _L0_ffn_ref(input_embeddings, router_w, w1, b1, w2, b2):
        import jax, jax.numpy as jnp
        import numpy as np
        NUM_EXPERTS = 8
        TOP_K = 2
        B, S, D = (8, 2048, 64)

        def _moe(tokens, router_w, w1, b1, w2, b2):
            N = tokens.shape[0]
            E = router_w.shape[0]
            logits = tokens.astype(jnp.float32) @ router_w.astype(jnp.float32).T
            probs = jax.nn.softmax(logits, axis=-1)
            rw, re = jax.lax.top_k(probs, TOP_K)
            if TOP_K > 1:
                rw = rw / jnp.maximum(rw.sum(-1, keepdims=True), 1e-12)
            rw = rw.astype(tokens.dtype)
            combine = jnp.zeros((N, E), tokens.dtype).at[jnp.arange(N)[:, None], re].set(rw)
            out = tokens
            for e in range(E):
                h = jax.nn.gelu(tokens @ w1[e] + b1[e], approximate=False)
                y = h @ w2[e] + b2[e]
                out = out + combine[:, e:e + 1] * y
            return out
        b, s, d = input_embeddings.shape
        tokens = input_embeddings.reshape(b * s, d)
        return _moe(tokens, router_w, w1, b1, w2, b2).reshape(b, s, d)

    def _L1_conv_ref(x, kernel):
        import jax, jax.numpy as jnp
        import numpy as np
        H_CONST = 1.0

        def binarize(w, H=H_CONST):
            return jnp.where(w >= 0, H, -H).astype(w.dtype)
        Wb = binarize(kernel)
        out = jax.lax.conv_general_dilated(x, Wb, window_strides=(1, 1), padding='SAME', dimension_numbers=('NHWC', 'HWIO', 'NHWC'))
        return out

    def _L1_ffn_ref(x, gate_w, gate_b, W1, b1, W2, b2):
        import jax, jax.numpy as jnp
        import numpy as np
        B, T, D, H, E = (16, 1024, 64, 128, 8)
        Bb, Tt, Dd = x.shape
        Ee = gate_w.shape[1]
        xf = x.reshape(-1, Dd)
        N = xf.shape[0]
        logits = xf @ gate_w + gate_b
        probs = jax.nn.softmax(logits, axis=-1)
        top2_vals, top2_idx = jax.lax.top_k(probs, 2)
        cw = jnp.zeros((N, Ee), dtype=xf.dtype).at[jnp.arange(N)[:, None], top2_idx].add(top2_vals)

        def step(acc, params):
            w1, bb1, w2, bb2, we = params
            h = jax.nn.gelu(xf @ w1 + bb1, approximate=False)
            y = h @ w2 + bb2
            return (acc + we[:, None] * y, None)
        out, _ = jax.lax.scan(step, jnp.zeros_like(xf), (W1, b1, W2, b2, cw.T))
        return out.reshape(Bb, Tt, Dd)

    def _gn(v, G=32, eps=1e-05):
        B_, H_, W_, C_ = v.shape
        g = v.reshape(B_, H_, W_, G, C_ // G)
        m = jnp.mean(g, axis=(1, 2, 4), keepdims=True)
        s = jnp.var(g, axis=(1, 2, 4), keepdims=True)
        return ((g - m) / jnp.sqrt(s + eps)).reshape(v.shape)

    def _ln_c(v, eps=1e-06):
        m = jnp.mean(v, axis=-1, keepdims=True)
        s = jnp.var(v, axis=-1, keepdims=True)
        return (v - m) / jnp.sqrt(s + eps)

    def _ln_t(v, eps=1e-05):
        m = jnp.mean(v, axis=-1, keepdims=True)
        s = jnp.var(v, axis=-1, keepdims=True)
        return (v - m) / jnp.sqrt(s + eps)

    def _to_tokens(v):
        B_, H_, W_, C_ = v.shape
        return v.reshape(B_, H_ * W_, C_)

    def _from_tokens(t, like):
        return t.reshape(like.shape)
    x = x + _L0_conv_ref(_ln_c(x), L0_conv_qkv_w, L0_conv_qkv_b, L0_conv_lepe_w, L0_conv_lepe_b, L0_conv_out_w, L0_conv_out_b)
    t = _to_tokens(x)
    t = t + _L0_ffn_ref(_ln_t(t), L0_ffn_router_w, L0_ffn_w1, L0_ffn_b1, L0_ffn_w2, L0_ffn_b2)
    x = _from_tokens(t, x)
    x = x + _L1_conv_ref(_ln_c(x), L1_conv_kernel)
    t = _to_tokens(x)
    t = t + _L1_ffn_ref(_ln_t(t), L1_ffn_gate_w, L1_ffn_gate_b, L1_ffn_W1, L1_ffn_b1, L1_ffn_W2, L1_ffn_b2)
    x = _from_tokens(t, x)
    return x

_drawn_inputs = setup_inputs


def setup_inputs(seed=0):
    import zlib

    import numpy as np

    out = dict(_drawn_inputs(seed))
    spreads = {'L0_ffn_b1': (0.0, 0.336),
     'L0_ffn_b2': (0.0, 0.1),
     'L1_ffn_gate_b': (0.0, 2.0),
     'L1_ffn_b1': (0.0, 2.0),
     'L1_ffn_b2': (0.0, 2.0)}
    factors = {'L1_ffn_gate_w': 8.0, 'L1_ffn_W1': 8.0, 'L1_ffn_W2': 8.0}
    for name, (base, spread) in spreads.items():
        noise = np.random.default_rng([zlib.crc32(name.encode()), seed]).standard_normal(out[name].shape)
        drawn = base * np.exp(spread * noise) if base else spread * noise
        out[name] = jnp.asarray(drawn.astype(out[name].dtype))
    for name, factor in factors.items():
        out[name] = (out[name] * factor).astype(out[name].dtype)
    return out
```

```python
import concourse.bass as bass
from concourse import mybir
from contextlib import ExitStack

F32 = mybir.dt.float32
U32 = mybir.dt.uint32
ALU = mybir.AluOpType
ACT = mybir.ActivationFunctionType
AX = mybir.AxisListType

B, H, W, C = 8, 56, 56, 64
NWIN = 7
REG = NWIN * NWIN
RH = H // NWIN
RTOK = RH * RH
NHEAD, HD, TOPK = 8, 8, 4
NKEY = TOPK * RTOK
KSEL = NKEY // 8
HP = NHEAD // 2
STRIP = RH * W
NSTRIP = B * NWIN
TILE, NT = 112, 4
NE = 8
PW = W + 2
NREG = B * REG
PAIR_REG = 2 * NWIN
RING = 7
AHEAD = 4
GONE = -3.0e38
KV1 = 2 * C + 1


def program(nc, x, out, w):
    ctx = ExitStack()
    with ctx:
        def sb(name, shape, dt=F32):
            return ctx.enter_context(nc.sbuf_tensor(name, shape, dt))

        def pb(name):
            return ctx.enter_context(nc.psum_tensor(name, [128, 512], F32))

        ahead = []

        def sem(name, start=0):
            s = ctx.enter_context(nc.semaphore(name))
            if start:
                ahead.append((s, start))
            return s

        def sems(name, n, start=0):
            return [sem(f"{name}{k}", start) for k in range(n)]

        def alone(eng):
            eng.sem_inc(passed[eng.engine], 1)

        def split(eng, n, by):
            return (n // by, n % by) if isinstance(n, int) else (eng.snap(n // by), eng.snap(n % by))

        def dram(name, shape, dt=F32):
            return nc.dram_tensor(name, shape, dt).ap()

        q_d = dram("q_d", [NREG, C, RTOK])
        kv_d = dram("kv_d", [NREG, RTOK, 2 * C])
        qr_d = dram("qr_d", [NSTRIP, C, NWIN])
        kr_d = dram("kr_d", [B, C, REG])
        idx_d = dram("idx_d", [NREG, 8], U32)
        vpad_d = dram("vpad_d", [B, C, PW, PW])
        at_d = dram("at_d", [NSTRIP, 32, 2 * STRIP])
        x2_d = dram("x2_d", [NSTRIP, TILE, NT * C])
        cpad_d = dram("cpad_d", [B, C, PW, PW])

        x_s = x.rearrange("b y x c -> (b y x) c").rearrange("(s t p) c -> s p t c", t=NT, p=TILE)
        out_s = out.rearrange("b y x c -> (b y x) c").rearrange("(s t p) c -> s p t c", t=NT, p=TILE)

        k = {name: sb("k_" + name, list(ap.shape)) for name, ap in w.items()}
        lepe_tap = sb("lepe_tap", [C, 9, C])
        conv_tap = sb("conv_tap", [C, 9, C])
        out_bias = sb("out_bias", [C, 1])
        zpad = sb("zpad", [C, B, PW])

        a_x = [sb(f"a_x{i}", [TILE, NT, C]) for i in range(2)]
        a_st = [sb(f"a_st{i}", [TILE, NT, 6]) for i in range(2)]
        a_mv = [sb(f"a_mv{i}", [TILE, NT, 2]) for i in range(2)]
        a_rs = [sb(f"a_rs{i}", [TILE, NT]) for i in range(2)]
        a_xn = [sb(f"a_xn{i}", [TILE, NT, C]) for i in range(2)]
        a_xT = [sb(f"a_xT{i}", [C + 1, STRIP]) for i in range(2)]
        a_qk = [sb(f"a_qk{i}", [128, NWIN, RTOK]) for i in range(2)]
        a_v = [sb(f"a_v{i}", [RTOK, NWIN, C]) for i in range(2)]
        a_vT = [sb(f"a_vT{i}", [C, RH, PW]) for i in range(2)]
        a_sum = [sb(f"a_sum{i}", [128, NWIN]) for i in range(2)]

        t_q = [sb(f"t_q{i}", [C, NWIN]) for i in range(2)]
        t_k = [sb(f"t_k{i}", [C, REG]) for i in range(2)]
        t_a = [sb(f"t_a{i}", [NWIN, REG]) for i in range(2)]
        t_v = [sb(f"t_v{i}", [NWIN, 8]) for i in range(2)]
        t_i = [sb(f"t_i{i}", [NWIN, 8], U32) for i in range(2)]

        b_kv = [sb(f"b_kv{i}", [128, 2, KV1]) for i in range(RING)]
        b_q = [sb(f"b_q{i}", [128, RTOK]) for i in range(RING)]
        b_qe = [sb(f"b_qe{i}", [128, NHEAD, RTOK]) for i in range(2)]
        b_s = [sb(f"b_s{i}", [128, HP, NKEY]) for i in range(2)]
        b_r = [sb(f"b_r{i}", [128, HP, NKEY]) for i in range(2)]
        b_e = [sb(f"b_e{i}", [128, HP, NKEY]) for i in range(2)]
        b_v8 = [sb(f"b_v8{i}", [128, HP, KSEL]) for i in range(2)]
        b_nm = [sb(f"b_nm{i}", [128, HP]) for i in range(2)]
        b_pT = [sb(f"b_pT{i}", [128, 512]) for i in range(2)]
        b_o = sb("b_o", [128, HD + HP * (C + 1 + 2 * HD)])
        b_rec = sb("b_rec", [128, HP])
        b_on = sb("b_on", [128, HP, HD])
        b_at = [sb(f"b_at{i}", [32, 2, RH, W]) for i in range(2)]

        c_x = [sb(f"c_x{i}", [TILE, NT, C]) for i in range(2)]
        c_at = [sb(f"c_at{i}", [32, 2, STRIP]) for i in range(2)]
        c_win = [sb(f"c_win{i}", [C, RH + 2, PW]) for i in range(2)]
        c_yT = sb("c_yT", [C, STRIP])
        c_tok = sb("c_tok", [TILE, NT, C])
        c_st = sb("c_st", [TILE, NT, 6])
        c_mv = sb("c_mv", [TILE, NT, 2])
        c_rs = sb("c_rs", [TILE, NT])
        c_xn = sb("c_xn", [TILE, NT, C])
        c_xr = sb("c_xr", [TILE, NT, C])
        c_xT = sb("c_xT", [C + 1, STRIP])
        c_lm = sb("c_lm", [TILE, NT])
        c_l = sb("c_l", [TILE, NT, NE])
        c_p = sb("c_p", [TILE, NT, NE])
        c_z = sb("c_z", [TILE, NT])
        c_rz = sb("c_rz", [TILE, NT])
        c_pv = sb("c_pv", [TILE, NT, 8])
        c_pi = sb("c_pi", [TILE, NT, 8], U32)
        c_pf = sb("c_pf", [TILE, NT, 8])
        c_m = [sb(f"c_m{i}", [TILE, NT, NE]) for i in range(2)]
        c_cw = sb("c_cw", [TILE, NT, NE])
        c_cwT = sb("c_cwT", [NE, STRIP])
        c_h = [sb(f"c_h{i}", [128, STRIP]) for i in range(2)]
        c_cb = [sb(f"c_cb{i}", [128, STRIP]) for i in range(2)]
        c_x2 = sb("c_x2", [TILE, NT, C])
        c_xp = sb("c_xp", [C, RH, PW])

        s_ps = [pb("s_ps0"), pb("s_ps1")]
        pT_ps, o_ps, a_ps = pb("pT_ps"), pb("o_ps"), pb("a_ps")
        y_ps, h_ps, g_ps = pb("y_ps"), pb("h_ps"), pb("g_ps")

        passed = {e.engine: ctx.enter_context(nc.semaphore(f"passed_{n}")) for n, e in
                  (("pe", nc.tensor), ("act", nc.scalar), ("dve", nc.vector), ("pool", nc.gpsimd), ("sp", nc.sync))}
        w_in, w_dve, w_pe, w_pool, pad_out = sem("w_in"), sem("w_dve"), sem("w_pe"), sem("w_pool"), sem("pad_out")
        a_in = sems("a_in", 2)
        a_stat = sem("a_stat")
        a_bn = sem("a_bn")
        a_tmp = sem("a_tmp")
        a_rstd = sem("a_rstd")
        a_norm = sem("a_norm", 2)
        a_full = sem("a_full")
        a_ev = sem("a_ev", 8)
        a_pool = sem("a_pool", 2)
        a_out = sems("a_out", 2, 5 * 16)
        t_in = sems("t_in", 2)
        t_full, t_ev, t_max, t_idx = sem("t_full"), sem("t_ev", 2), sem("t_max"), sem("t_idx", 2)
        t_out = sems("t_out", 2, 16)
        b_in = sems("b_in", RING)
        b_qx = sem("b_qx")
        b_qk = sem("b_qk", 2)
        b_sc = sem("b_sc", 1)
        b_chain = sem("b_chain")
        b_sel = sem("b_sel")
        b_neg = sem("b_neg")
        b_exp = sem("b_exp", 2)
        b_msk = sem("b_msk")
        b_prob = sem("b_prob", 2)
        b_pt = sem("b_pt")
        b_ptc = sem("b_ptc", 1)
        b_pv = sem("b_pv", RING)
        b_oc = sem("b_oc")
        b_rc = sem("b_rc")
        b_nrm = sem("b_nrm", 1)
        b_ot = sem("b_ot", 1)
        b_att = sem("b_att", 1)
        b_out = sems("b_out", 2, 16)
        cs = []
        for layer in (0, 1):
            n = f"c{layer}_"
            cs.append(dict(
                x_in=sems(n + "x_in", 2), free=sem(n + "free", 2),
                y=sem(n + "y"), yT=sem(n + "yT"), yt=sem(n + "yt", 1), x1=sem(n + "x1"), stat=sem(n + "stat"),
                tmp=sem(n + "tmp"), rstd=sem(n + "rstd"), norm=sem(n + "norm"), res=sem(n + "res"),
                xt=sem(n + "xt"), xT=sem(n + "xT"), lg=sem(n + "lg"), chain=sem(n + "chain"), ls=sem(n + "ls"),
                ex=sem(n + "ex"), top=sem(n + "top"), cw=sem(n + "cw"), ct=sem(n + "ct"), cT=sem(n + "cT"),
                h=sem(n + "h"), ge=sem(n + "ge", 1), cb=sem(n + "cb", 1), hc=sem(n + "hc"), used=sem(n + "used", 2),
                x2=sem(n + "x2", 1), out=sem(n + "out", 16), pout=sem(n + "pout", 16)))
            cs[-1].update(stat2=sem(n + "stat2"), rstd2=sem(n + "rstd2"), norm2=sem(n + "norm2"),
                          pt=sem(n + "pt"), pT=sem(n + "pT"))

        def stats(dve, src, st, mv, chain, chained, then):
            for t in range(NT):
                dve.bn_stats(out=st[:, t, :], in_=src[:, t, :]).then_inc(chain, 1)
            for t in range(NT):
                dve.wait_ge(chain, chained + t + 1)
                alone(dve)
                last = dve.bn_aggr(out=mv[:, t, :], in_=st[:, t, :])
            last.then_inc(then, 1)

        def rstd(pool, mv, rs, eps, tmp, tmped, then):
            pool.tensor_scalar(out=rs[:, :], in0=mv[:, :, 1], scalar1=eps, scalar2=1.0,
                               op0=ALU.add, op1=ALU.mult).then_inc(tmp, 1)
            pool.wait_ge(tmp, tmped + 1)
            pool.tensor_tensor(out=rs[:, :], in0=rs[:, :], in1=k["mhalf"][0:TILE, 0:NT],
                               op=ALU.pow).then_inc(then, 1)

        def normalise(dve, src, mv, rs, dst, then):
            for t in range(NT):
                last = dve.tensor_scalar(out=dst[:, t, :], in0=src[:, t, :], scalar1=mv[:, t, 0:1],
                                         scalar2=rs[:, t:t + 1], op0=ALU.subtract, op1=ALU.mult)
            last.then_inc(then, 1)

        def to_channels(pe, src, ps):
            for t in range(NT):
                last = pe.transpose(ps[0:C, t * TILE:(t + 1) * TILE], src[:, t, :], k["ident"][0:TILE, 0:TILE])
            return last

        def sp_a(sp, tau):
            for i in range(2):
                s = tau * 2 + i
                sp.wait_ge(a_norm, s + 1)
                sp.dma_start(a_x[i][:], x_s[bass.ds(s, 1)].rearrange("a p t c -> (a p) t c")).then_inc(a_in[i], 16)
            for i in range(2):
                s = tau * 2 + i
                b, y = split(sp, s, NWIN)
                put = a_out[i]
                sp.wait_ge(a_pool, s + 3)
                sp.dma_start(q_d[bass.ds(s * NWIN, NWIN)].rearrange("w c t -> c w t"), a_qk[i][0:C]).then_inc(put, 16)
                sp.dma_start(kv_d[bass.ds(s * NWIN, NWIN), :, 0:C].rearrange("w c t -> c w t"),
                             a_qk[i][C:128]).then_inc(put, 16)
                sp.dma_start(qr_d[bass.ds(s, 1)].rearrange("a c w -> (a c) w"), a_sum[i][0:C]).then_inc(put, 16)
                with nc.allow_non_contiguous_dma(reason="seven region sums a row"):
                    sp.dma_start(kr_d[bass.ds(b, 1), :, bass.ds(y * NWIN, NWIN)].rearrange("a c w -> (a c) w"),
                                 a_sum[i][C:128]).then_inc(put, 16)
                sp.wait_ge(a_ev, 4 * s + 12)
                sp.dma_start(kv_d[bass.ds(s * NWIN, NWIN), :, C:2 * C].rearrange("w t c -> t w c"),
                             a_v[i][:]).then_inc(put, 16)
                sp.dma_start(vpad_d[bass.ds(b, 1), :, bass.ds(y * RH + 1, RH), :].rearrange("a c h w -> (a c) h w"),
                             a_vT[i][:]).then_inc(put, 16)

        def dve_a(dve, tau):
            for i in range(2):
                s = tau * 2 + i
                dve.wait_ge(a_in[i], 16 * (tau + 1))
                dve.wait_ge(a_norm, s + 1)
                alone(dve)
                stats(dve, a_x[i], a_st[i], a_mv[i], a_bn, 4 * s, a_stat)
            for i in range(2):
                s = tau * 2 + i
                dve.wait_ge(a_rstd, s + 1)
                dve.wait_ge(a_ev, 4 * s + 1)
                alone(dve)
                normalise(dve, a_x[i], a_mv[i], a_rs[i], a_xn[i], a_norm)
            for i in range(2):
                s = tau * 2 + i
                dve.wait_ge(a_ev, 4 * s + 10)
                dve.wait_ge(a_out[i], 96 * tau + 80)
                dve.tensor_reduce(out=a_sum[i][:, :], in_=a_qk[i][:], op=ALU.add, axis=AX.X).then_inc(a_pool, 1)

        def pool_a(pool, tau):
            for i in range(2):
                s = tau * 2 + i
                pool.wait_ge(a_stat, s + 1)
                alone(pool)
                rstd(pool, a_mv[i], a_rs[i], 1e-6, a_tmp, s, a_rstd)

        def pe_a(pe, tau):
            for i in range(2):
                s = tau * 2 + i
                full = a_full
                pe.wait_ge(a_norm, s + 3)
                pe.wait_ge(a_ev, 4 * s + 8)
                alone(pe)
                to_channels(pe, a_xn[i], a_ps).then_inc(full, 1)
                pe.wait_ge(a_ev, 4 * s + 9)
                alone(pe)
                pe.matmul(a_ps[:, 0:STRIP], k["wqkv"][:, 0:128], a_xT[i][:, :], start=True, stop=True).then_inc(full, 1)
                pe.wait_ge(a_ev, 4 * s + 10)
                alone(pe)
                for r in range(NWIN):
                    last = pe.matmul(a_ps[0:RTOK, r * C:(r + 1) * C], a_xT[i][:, r * RTOK:(r + 1) * RTOK],
                                     k["wqkv"][:, 128:192], start=True, stop=True)
                last.then_inc(full, 1)
                pe.wait_ge(a_ev, 4 * s + 11)
                alone(pe)
                pe.matmul(a_ps[0:C, 0:STRIP], k["wqkv"][:, 128:192],
                          a_xT[i][:, :].rearrange("c (w h q) -> c h w q", w=NWIN, h=RH),
                          start=True, stop=True).then_inc(full, 1)

        def act_a(act, tau):
            for i in range(2):
                s = tau * 2 + i
                ev = a_ev
                act.wait_ge(a_full, 4 * s + 1)
                act.activation(a_xT[i][0:C, :].rearrange("c (w h q) -> c h w q", w=NWIN, h=RH),
                               a_ps[0:C, 0:STRIP].rearrange("c (h w q) -> c h w q", h=RH, w=NWIN), ACT.Copy).then_inc(ev, 1)
                act.wait_ge(a_out[i], 96 * tau + 80)
                act.wait_ge(a_full, 4 * s + 2)
                act.wait_ge(a_pool, s + 1)
                act.activation(a_qk[i][:].rearrange("c w t -> c (w t)"), a_ps[:, 0:STRIP], ACT.Copy).then_inc(ev, 1)
                act.wait_ge(a_full, 4 * s + 3)
                act.activation(a_v[i][:].rearrange("t w c -> t (w c)"), a_ps[0:RTOK, 0:STRIP], ACT.Copy).then_inc(ev, 1)
                act.wait_ge(a_full, 4 * s + 4)
                act.activation(a_vT[i][:, :, 1:W + 1], a_ps[0:C, 0:STRIP].rearrange("c (h w) -> c h w", h=RH),
                               ACT.Copy).then_inc(ev, 1)

        def sp_t(sp, tau):
            for i in range(2):
                s = tau * 2 + i
                b, _ = split(sp, s, NWIN)
                sp.wait_ge(t_ev, s + 1)
                sp.dma_start(t_q[i][:], qr_d[bass.ds(s, 1)].rearrange("a c w -> (a c) w")).then_inc(t_in[i], 16)
                sp.dma_start(t_k[i][:], kr_d[bass.ds(b, 1)].rearrange("a c w -> (a c) w")).then_inc(t_in[i], 16)
            for i in range(2):
                s = tau * 2 + i
                sp.wait_ge(t_idx, s + 3)
                sp.dma_start(idx_d[bass.ds(s * NWIN, NWIN)], t_i[i][:]).then_inc(t_out[i], 16)
            for i in range(2):
                sp.wait_ge(t_out[i], 16 * (tau + 1) + 16)
                alone(sp)

        def pe_t(pe, tau):
            for i in range(2):
                s = tau * 2 + i
                pe.wait_ge(t_in[i], 32 * (tau + 1))
                pe.wait_ge(t_ev, s + 2)
                alone(pe)
                pe.matmul(a_ps[0:NWIN, 0:REG], t_q[i][:, :], t_k[i][:, :], start=True, stop=True).then_inc(t_full, 1)

        def act_t(act, tau):
            for i in range(2):
                s = tau * 2 + i
                act.wait_ge(t_full, s + 1)
                act.wait_ge(t_idx, s + 1)
                act.activation(t_a[i][:, :], a_ps[0:NWIN, 0:REG], ACT.Copy).then_inc(t_ev, 1)

        def dve_t(dve, tau):
            for i in range(2):
                s = tau * 2 + i
                dve.wait_ge(t_ev, s + 3)
                alone(dve)
                dve.max(out=t_v[i][:, :], in_=t_a[i][:, :]).then_inc(t_max, 1)
                dve.wait_ge(t_out[i], 16 * tau + 16)
                dve.wait_ge(t_max, s + 1)
                alone(dve)
                dve.max_index(out=t_i[i][:, :], in_max=t_v[i][:, :], in_values=t_a[i][:, :]).then_inc(t_idx, 1)

        def sp_gather(sp, tau, r):
            reg, slot = tau * PAIR_REG + r, r % RING
            b, _ = split(sp, reg, REG)
            got = b_in[slot]
            sp.wait_ge(b_pv, reg - RING + 8)
            alone(sp)
            best = [sp.value_load(idx_d[bass.ds(reg, 1), j:j + 1], min_val=0, max_val=REG - 1) for j in range(TOPK)]
            for j in range(TOPK):
                src = sp.snap(best[j] + b * REG)
                half = (j % 2) * RTOK
                sp.dma_start(b_kv[slot][half:half + RTOK, j // 2, 0:2 * C],
                             kv_d[bass.ds(src, 1)].rearrange("a p c -> (a p) c")).then_inc(got, 16)
            for half in (0, C):
                sp.dma_start(b_q[slot][half:half + C, :], q_d[bass.ds(reg, 1)].rearrange("a c t -> (a c) t")).then_inc(got, 16)

        def pool_spread(pool, tau, r):
            reg = tau * PAIR_REG + r
            pool.wait_ge(b_in[r % RING], 96 * (tau * 2 + r // RING + 1))
            pool.wait_ge(b_qk, reg + 1)
            pool.tensor_tensor(out=b_qe[r % 2][:, :, :],
                               in0=b_q[r % RING][:, :].unsqueeze(1).broadcast_to([128, NHEAD, RTOK]),
                               in1=k["head"][:, :].unsqueeze(2).broadcast_to([128, NHEAD, RTOK]),
                               op=ALU.mult).then_inc(b_qx, 1)

        def pe_scores(pe, tau, r):
            reg = tau * PAIR_REG + r
            pe.wait_ge(b_in[r % RING], 96 * (tau * 2 + r // RING + 1))
            pe.wait_ge(b_qx, reg + 1)
            pe.wait_ge(b_sc, reg + 1)
            alone(pe)
            for half in range(2):
                part = slice(half * C, half * C + C)
                for t in range(HP):
                    last = pe.matmul(s_ps[half][:, t * 128:(t + 1) * 128],
                                     b_qe[r % 2][part, 2 * t:2 * t + 2, :].rearrange("c h t -> c (h t)"),
                                     b_kv[r % RING][part, :, 0:RTOK], start=True, stop=True)
            last.then_inc(b_qk, 1)

        def act_scores(act, tau, r):
            reg = tau * PAIR_REG + r
            act.wait_ge(b_exp, reg + 1)
            act.wait_ge(b_qk, reg + 3)
            for half in range(2):
                last = act.activation(b_s[r % 2][:].rearrange("p t (a h q) -> p h t a q", h=2, q=RTOK)[:, half],
                                      s_ps[half][:, :].rearrange("p (t a q) -> p t a q", t=HP, a=2), ACT.Copy)
            last.then_inc(b_sc, 1)

        def dve_select(dve, tau, r):
            reg, p = tau * PAIR_REG + r, r % 2
            chain = b_chain
            dve.wait_ge(b_sc, reg + 2)
            dve.wait_ge(b_prob, reg + 1)
            alone(dve)
            rounds = KSEL // 8
            for rnd in range(rounds):
                src = b_s[p] if rnd == 0 else b_r[p]
                for t in range(HP):
                    if rnd:
                        dve.wait_ge(chain, (2 * rnd - 1) * HP + t + 1)
                        alone(dve)
                    dve.max(out=b_v8[p][:, t, 8 * rnd:8 * rnd + 8], in_=src[:, t, :]).then_inc(chain, 1)
                for t in range(HP):
                    dve.wait_ge(chain, 2 * rnd * HP + t + 1)
                    last = dve.match_replace(out=b_r[p][:, t, :], in_to_replace=b_v8[p][:, t, 8 * rnd:8 * rnd + 8],
                                             in_values=src[:, t, :], imm_value=GONE)
                    if rnd < rounds - 1:
                        last.then_inc(chain, 1)
            last.then_inc(b_sel, 1)
            dve.sem_clear(chain)

        def dve_recip(dve, tau, r):
            reg = tau * PAIR_REG + r
            dve.wait_ge(b_oc, reg + 1)
            dve.wait_ge(b_nrm, reg + 1)
            dve.reciprocal(b_rec[:, :], b_o[:, 0:HP * (C + 1)].rearrange("p (t c) -> p t c", t=HP)[:, :, C]).then_inc(b_rc, 1)

        def act_exp(act, tau, r):
            reg, p = tau * PAIR_REG + r, r % 2
            act.wait_ge(b_sel, reg + 1)
            act.activation(b_nm[p][:, :], b_v8[p][:, :, 0], ACT.Copy, scale=-1.0).then_inc(b_neg, 1)
            act.wait_ge(b_prob, reg + 1)
            act.wait_ge(b_neg, reg + 1)
            for t in range(HP):
                last = act.activation(b_e[p][:, t, :], b_s[p][:, t, :], ACT.Exp, bias=b_nm[p][:, t:t + 1])
            last.then_inc(b_exp, 1)

        def pool_mask(pool, tau, r):
            reg, p = tau * PAIR_REG + r, r % 2
            pool.wait_ge(b_nrm, reg + 1)
            pool.wait_ge(b_sel, reg + 1)
            alone(pool)
            pool.tensor_scalar(out=b_r[p][:, :, :], in0=b_r[p][:, :, :], scalar1=GONE, scalar2=None,
                               op0=ALU.is_le).then_inc(b_msk, 1)

        def pool_prob(pool, tau, r):
            reg, p = tau * PAIR_REG + r, r % 2
            pool.wait_ge(b_msk, reg + 1)
            pool.wait_ge(b_exp, reg + 3)
            pool.tensor_tensor(out=b_e[p][:, :, :], in0=b_e[p][:, :, :], in1=b_r[p][:, :, :],
                               op=ALU.mult).then_inc(b_prob, 1)

        def pe_values(pe, tau, r):
            reg, p = tau * PAIR_REG + r, r % 2
            pe.wait_ge(b_prob, reg + 3)
            alone(pe)
            for half in range(2):
                pe.wait_ge(b_ptc, 2 * reg + half + 1)
                alone(pe)
                for t in range(2 * half, 2 * half + 2):
                    for c in range(2):
                        col = (t % 2) * 256 + c * 128
                        last = pe.transpose(pT_ps[:, col:col + 128], b_e[p][:, t, c * 128:(c + 1) * 128], k["ident"][:, :])
                last.then_inc(b_pt, 1)
            pe.wait_ge(b_att, reg + 1)
            alone(pe)
            for t in range(HP):
                if t % 2 == 0:
                    pe.wait_ge(b_ptc, 2 * reg + t // 2 + 2)
                    alone(pe)
                for c in range(2):
                    last = pe.matmul(o_ps[:, t * (C + 1):(t + 1) * (C + 1)],
                                     b_pT[t // 2][:, (t % 2) * 256 + c * 128:(t % 2) * 256 + (c + 1) * 128],
                                     b_kv[r % RING][:, c, C:KV1], start=(c == 0), stop=(c == 1))
            last.then_inc(b_pv, 1)

        def act_values(act, tau, r):
            reg = tau * PAIR_REG + r
            act.wait_ge(b_pv, reg + 7)
            for half in range(2):
                act.wait_ge(b_pt, 2 * reg + half + 1)
                act.activation(b_pT[half][:, :], pT_ps[:, :], ACT.Copy).then_inc(b_ptc, 1)
            act.wait_ge(b_nrm, reg + 1)
            act.wait_ge(b_pv, reg + 8)
            act.activation(b_o[:, 0:HP * (C + 1)], o_ps[:, 0:HP * (C + 1)], ACT.Copy).then_inc(b_oc, 1)

        def pool_norm(pool, tau, r):
            reg = tau * PAIR_REG + r
            pool.wait_ge(b_rc, reg + 1)
            pool.wait_ge(b_ot, reg + 1)
            pool.wait_ge(b_prob, reg + 3)
            step = C + 1 + 2 * HD
            for half in range(2):
                part = slice(half * RTOK, half * RTOK + RTOK)
                own = b_o[part, half * HD:half * HD + HP * step].rearrange("p (t c) -> p t c", c=step)[:, :, 0:HD]
                last = pool.tensor_tensor(out=b_on[part, :, :], in0=own,
                                          in1=b_rec[part, :].unsqueeze(2).broadcast_to([RTOK, HP, HD]), op=ALU.mult)
            last.then_inc(b_nrm, 1)

        def pe_out(pe, tau, r):
            reg = tau * PAIR_REG + r
            pe.wait_ge(b_nrm, reg + 2)
            alone(pe)
            pe.transpose(o_ps[0:32, 0:128], b_on[:, :, :].rearrange("p t c -> p (t c)"), k["ident"][:, :]).then_inc(b_ot, 1)

        def act_out(act, tau, r):
            reg, i, win = tau * PAIR_REG + r, (r // NWIN) % 2, r % NWIN
            if win == 0:
                act.wait_ge(b_out[i], 16 * tau + 16)
            act.wait_ge(b_ot, reg + 2)
            act.activation(b_at[i][:, :, :, win * RH:(win + 1) * RH],
                           o_ps[0:32, 0:128].rearrange("c (j h q) -> c j h q", j=2, h=RH), ACT.Copy).then_inc(b_att, 1)

        def sp_strip(sp, tau, i):
            s = tau * 2 + i
            sp.wait_ge(b_att, NWIN * (s + 1) + 1)
            sp.dma_start(at_d[bass.ds(s, 1)].rearrange("a c f -> (a c) f"),
                         b_at[i][:].rearrange("c j h w -> c (j h w)")).then_inc(b_out[i], 16)

        def sp_b(sp, tau, first=False, last=False):
            if first:
                for r in range(AHEAD):
                    sp_gather(sp, tau, r)
            for r in range(PAIR_REG):
                if r + AHEAD < PAIR_REG or not last:
                    sp_gather(sp, tau, r + AHEAD)
                if r == 0 and not first:
                    sp_strip(sp, tau - 1, 1)
                if r == NWIN:
                    sp_strip(sp, tau, 0)
            if last:
                sp_strip(sp, tau, 1)

        def pool_b(pool, tau, first=False, last=False):
            if first:
                pool_spread(pool, tau, 0)
                pool_spread(pool, tau, 1)
            for r in range(PAIR_REG):
                if r:
                    pool_norm(pool, tau, r - 1)
                elif not first:
                    pool_norm(pool, tau - 1, PAIR_REG - 1)
                pool_mask(pool, tau, r)
                if r + 2 < PAIR_REG or not last:
                    pool_spread(pool, tau, r + 2)
                pool_prob(pool, tau, r)
            if last:
                pool_norm(pool, tau, PAIR_REG - 1)

        def pe_b(pe, tau, first=False, last=False):
            if first:
                pe_scores(pe, tau, 0)
                pe_scores(pe, tau, 1)
            for r in range(PAIR_REG):
                if r + 2 < PAIR_REG or not last:
                    pe_scores(pe, tau, r + 2)
                if r:
                    pe_out(pe, tau, r - 1)
                elif not first:
                    pe_out(pe, tau - 1, PAIR_REG - 1)
                pe_values(pe, tau, r)
            if last:
                pe_out(pe, tau, PAIR_REG - 1)

        def act_b(act, tau, first=False, last=False):
            if first:
                act_scores(act, tau, 0)
                act_scores(act, tau, 1)
            for r in range(PAIR_REG):
                act_exp(act, tau, r)
                if r:
                    act_out(act, tau, r - 1)
                elif not first:
                    act_out(act, tau - 1, PAIR_REG - 1)
                if r + 2 < PAIR_REG or not last:
                    act_scores(act, tau, r + 2)
                act_values(act, tau, r)
            if last:
                act_out(act, tau, PAIR_REG - 1)

        def dve_b(dve, tau, first=False, last=False):
            for r in range(PAIR_REG):
                dve_select(dve, tau, r)
                if r:
                    dve_recip(dve, tau, r - 1)
                elif not first:
                    dve_recip(dve, tau - 1, PAIR_REG - 1)
            if last:
                dve_recip(dve, tau, PAIR_REG - 1)

        groups = (NE // 2, NE)
        w1, w2, b1, b2 = (k["w1_0"], k["w1_1"]), (k["w2_0"], k["w2_1"]), (k["b1_0"], k["b1_1"]), (k["b2_0"], k["b2_1"])
        sel, gate = (k["sel_0"], k["sel_1"]), (k["gate_0"], k["gate_1"])

        def sp_c(sp, tau, layer):
            S = cs[layer]
            for i in range(2):
                s = tau * 2 + i
                b, y = split(sp, s, NWIN)
                got = S["x_in"][i]
                sp.wait_ge(S["free"], s + 1)
                alone(sp)
                src = x_s[bass.ds(s, 1)].rearrange("a p t c -> (a p) t c") if layer == 0 else \
                    x2_d[bass.ds(s, 1)].rearrange("a p (t c) -> (a p) t c", t=NT)
                sp.dma_start(c_x[i][:], src).then_inc(got, 16)
                pad = vpad_d if layer == 0 else cpad_d
                sp.dma_start(c_win[i][:], pad[bass.ds(b, 1), :, bass.ds(y * RH, RH + 2), :].rearrange("a c h w -> (a c) h w")).then_inc(got, 16)
                if layer == 0:
                    sp.dma_start(c_at[i][:], at_d[bass.ds(s, 1)].rearrange("a c (j f) -> (a c) j f", j=2)).then_inc(got, 16)
            for i in range(2):
                s = tau * 2 + i
                b, y = split(sp, s, NWIN)
                sp.wait_ge(S["x2"], s + 2)
                alone(sp)
                dst = x2_d[bass.ds(s, 1)].rearrange("a p (t c) -> (a p) t c", t=NT) if layer == 0 else \
                    out_s[bass.ds(s, 1)].rearrange("a p t c -> (a p) t c")
                sp.dma_start(dst, c_x2[:]).then_inc(S["out"], 16)
                if layer == 0:
                    sp.wait_ge(S["pT"], s + 1)
                    sp.dma_start(cpad_d[bass.ds(b, 1), :, bass.ds(y * RH + 1, RH), :].rearrange("a c h w -> (a c) h w"),
                                 c_xp[:]).then_inc(S["pout"], 16)

        def pe_c(pe, tau, layer):
            S, G = cs[layer], groups[layer]
            for i in range(2):
                s = tau * 2 + i
                pe.wait_ge(S["x_in"][i], (48, 32)[layer] * (tau + 1))
                alone(pe)
                if layer == 0:
                    pe.wait_ge(S["x2"], s + 1)
                    alone(pe)
                else:
                    pe.wait_ge(S["x2"], s + 1)
                    alone(pe)
                taps = lepe_tap if layer == 0 else conv_tap
                for j in range(9):
                    last = pe.matmul(y_ps[0:C, 0:STRIP], taps[:, j, :], c_win[i][:, j // 3:j // 3 + RH, j % 3:j % 3 + W],
                                     start=(j == 0), stop=(j == 8 and layer == 1))
                if layer == 0:
                    for j in range(2):
                        last = pe.matmul(y_ps[0:C, 0:STRIP], k["outeo"][:, j, :], c_at[i][:, j, :], start=False, stop=(j == 1))
                last.then_inc(S["y"], 1)
                pe.wait_ge(S["yT"], s + 1)
                alone(pe)
                for t in range(NT):
                    last = pe.transpose(h_ps[0:TILE, t * C:(t + 1) * C], c_yT[:, t * TILE:(t + 1) * TILE], k["ident"][0:C, 0:C])
                last.then_inc(S["yt"], 1)
                pe.wait_ge(S["norm"], s + 1)
                alone(pe)
                to_channels(pe, c_xn, g_ps).then_inc(S["xt"], 1)
                pe.wait_ge(S["xT"], s + 1)
                alone(pe)
                for t in range(NT):
                    last = pe.matmul(h_ps[0:TILE, t * NE:(t + 1) * NE], c_xT[:, t * TILE:(t + 1) * TILE], gate[layer][:, :],
                                     start=True, stop=True)
                last.then_inc(S["lg"], 1)
                pe.wait_ge(S["cw"], s + 1)
                alone(pe)
                for t in range(NT):
                    last = pe.transpose(h_ps[0:NE, t * TILE:(t + 1) * TILE], c_cw[:, t, :], k["ident"][0:TILE, 0:TILE])
                last.then_inc(S["ct"], 1)
                pe.wait_ge(S["cT"], s + 1)
                alone(pe)

                def up(g):
                    n = s * G + g
                    pe.wait_ge(S["ge"], n + 1)
                    alone(pe)
                    pe.matmul(h_ps[:, 0:STRIP], w1[layer][:, g, :], c_xT[0:C, :], start=True, stop=True).then_inc(S["h"], 1)
                    pe.wait_ge(S["cb"], n + 1)
                    alone(pe)
                    pe.matmul(g_ps[:, 0:STRIP], sel[layer][:, g, :], c_cwT[:, :], start=True, stop=True).then_inc(S["h"], 1)

                up(0)
                for t in range(NT):
                    pe.matmul(y_ps[0:TILE, t * C:(t + 1) * C], c_cwT[:, t * TILE:(t + 1) * TILE], b2[layer][:, :],
                              start=(t == 0), stop=False, skip_group_check=True)
                for g in range(G):
                    if g + 1 < G:
                        up(g + 1)
                    pe.wait_ge(S["hc"], s * G + g + 1)
                    alone(pe)
                    for t in range(NT):
                        last = pe.matmul(y_ps[0:TILE, t * C:(t + 1) * C], c_h[g % 2][:, t * TILE:(t + 1) * TILE],
                                         w2[layer][:, g, :], start=False, stop=(g == G - 1), skip_group_check=True)
                    last.then_inc(S["used"], 1)
                if layer == 0:
                    pe.wait_ge(S["norm2"], s + 1)
                    alone(pe)
                    to_channels(pe, c_xn, g_ps).then_inc(S["pt"], 1)

        def act_c(act, tau, layer):
            S, G = cs[layer], groups[layer]
            func = (ACT.Gelu, ACT.Gelu_apprx_tanh)[layer]
            for i in range(2):
                s = tau * 2 + i
                act.wait_ge(S["y"], s + 1)
                act.wait_ge(S["yt"], s + 1)
                if layer == 0:
                    act.activation(c_yT[:, :], y_ps[0:C, 0:STRIP], ACT.Identity, bias=out_bias[:, 0:1]).then_inc(S["yT"], 1)
                else:
                    act.activation(c_yT[:, :], y_ps[0:C, 0:STRIP], ACT.Copy).then_inc(S["yT"], 1)
                act.wait_ge(S["xt"], s + 1)
                act.activation(c_xT[0:C, :], g_ps[0:C, 0:STRIP], ACT.Copy).then_inc(S["xT"], 1)
                act.wait_ge(S["ls"], s + 1)
                act.activation(c_p[:, :, :], c_l[:, :, :], ACT.Exp).then_inc(S["ex"], 1)
                act.wait_ge(S["ct"], s + 1)
                act.activation(c_cwT[:, :], h_ps[0:NE, 0:STRIP], ACT.Copy).then_inc(S["cT"], 1)
                for g in range(G):
                    n = s * G + g
                    act.wait_ge(S["used"], n + 1)
                    act.wait_ge(S["h"], 2 * n + 1)
                    act.activation(c_h[g % 2][:, :], h_ps[:, 0:STRIP], func, bias=b1[layer][:, g:g + 1]).then_inc(S["ge"], 1)
                    act.wait_ge(S["h"], 2 * n + 2)
                    act.activation(c_cb[g % 2][:, :], g_ps[:, 0:STRIP], ACT.Copy).then_inc(S["cb"], 1)
                if layer == 0:
                    act.wait_ge(S["pt"], s + 1)
                    act.wait_ge(S["pout"], 16 * s + 16)
                    act.activation(c_xp[:, :, 1:W + 1], g_ps[0:C, 0:STRIP].rearrange("c (h w) -> c h w", h=RH),
                                   ACT.Copy).then_inc(S["pT"], 1)

        def pool_c(pool, tau, layer):
            S, G = cs[layer], groups[layer]
            for i in range(2):
                s = tau * 2 + i
                pool.wait_ge(S["stat"], s + 1)
                alone(pool)
                rstd(pool, c_mv, c_rs, 1e-5, S["tmp"], (2 - layer) * s, S["rstd"])
                if layer == 0:
                    pool.wait_ge(S["norm"], s + 1)
                    pool.tensor_tensor(out=c_xr[:, :, :], in0=c_tok[:, :, :], in1=c_xn[:, :, :], op=ALU.add).then_inc(S["res"], 1)
                for g in range(G):
                    n = s * G + g
                    pool.wait_ge(S["cb"], n + 2)
                    pool.tensor_tensor(out=c_h[g % 2][:, :], in0=c_h[g % 2][:, :], in1=c_cb[g % 2][:, :], op=ALU.mult).then_inc(S["hc"], 1)
                if layer == 0:
                    pool.wait_ge(S["stat2"], s + 1)
                    alone(pool)
                    rstd(pool, c_mv, c_rs, 1e-6, S["tmp"], 2 * s + 1, S["rstd2"])

        def dve_c(dve, tau, layer):
            S, G = cs[layer], groups[layer]
            for i in range(2):
                s = tau * 2 + i
                count = [0]

                def link(ins):
                    count[0] += 1
                    ins.then_inc(S["chain"], 1)
                    dve.wait_ge(S["chain"], count[0])

                def mean_var(src, then):
                    for t in range(NT):
                        ins = dve.bn_stats(out=c_st[:, t, :], in_=src[:, t, :])
                        if t < NT - 1:
                            ins.then_inc(S["chain"], 1)
                            count[0] += 1
                    link(ins)
                    for t in range(NT):
                        ins = dve.bn_aggr(out=c_mv[:, t, :], in_=c_st[:, t, :])
                    ins.then_inc(then, 1)

                dve.sem_clear(S["chain"])
                dve.wait_ge(S["x_in"][i], (48, 32)[layer] * (tau + 1))
                dve.wait_ge(S["yt"], s + 2)
                alone(dve)
                link(dve.tensor_tensor(out=c_tok[:, :, :], in0=c_x[i][:, :, :],
                                       in1=h_ps[0:TILE, 0:NT * C].rearrange("p (t c) -> p t c", t=NT), op=ALU.add))
                dve.sem_inc(S["free"], 1)
                mean_var(c_tok, S["stat"])
                dve.wait_ge(S["rstd"], s + 1)
                alone(dve)
                normalise(dve, c_tok, c_mv, c_rs, c_xn, S["norm"])
                dve.wait_ge(S["lg"], s + 1)
                alone(dve)
                lg = h_ps[0:TILE, 0:NT * NE].rearrange("p (t e) -> p t e", t=NT)
                link(dve.tensor_reduce(out=c_lm[:, :], in_=lg, op=ALU.max, axis=AX.X))
                dve.tensor_tensor(out=c_l[:, :, :], in0=lg, in1=c_lm[:, :].unsqueeze(2).broadcast_to([TILE, NT, NE]),
                                  op=ALU.subtract).then_inc(S["ls"], 1)
                dve.wait_ge(S["ex"], s + 1)
                alone(dve)
                link(dve.tensor_reduce(out=c_z[:, :], in_=c_p[:, :, :], op=ALU.add, axis=AX.X))
                link(dve.reciprocal(c_rz[:, :], c_z[:, :]))
                link(dve.tensor_tensor(out=c_p[:, :, :], in0=c_p[:, :, :], in1=c_rz[:, :].unsqueeze(2).broadcast_to([TILE, NT, NE]), op=ALU.mult))
                for t in range(NT):
                    ins = dve.max(out=c_pv[:, t, :], in_=c_p[:, t, :])
                link(ins)
                for t in range(NT):
                    ins = dve.max_index(out=c_pi[:, t, :], in_max=c_pv[:, t, :], in_values=c_p[:, t, :])
                link(ins)
                link(dve.tensor_copy(c_pf[:, :, :], c_pi[:, :, :]))
                for j in range(2):
                    ins = dve.tensor_tensor(out=c_m[j][:, :, :], in0=k["iota"][0:TILE, :].unsqueeze(1).broadcast_to([TILE, NT, NE]),
                                            in1=c_pf[:, :, j:j + 1].broadcast_to([TILE, NT, NE]), op=ALU.is_equal)
                link(ins)
                link(dve.tensor_tensor(out=c_m[0][:, :, :], in0=c_m[0][:, :, :], in1=c_m[1][:, :, :], op=ALU.add))
                ins = dve.tensor_tensor(out=c_cw[:, :, :], in0=c_m[0][:, :, :], in1=c_p[:, :, :], op=ALU.mult)
                if layer == 0:
                    link(ins)
                    link(dve.tensor_tensor(out=c_z[:, :], in0=c_pv[:, :, 0], in1=c_pv[:, :, 1], op=ALU.add))
                    link(dve.tensor_scalar(out=c_z[:, :], in0=c_z[:, :], scalar1=1e-12, scalar2=None, op0=ALU.max))
                    link(dve.reciprocal(c_rz[:, :], c_z[:, :]))
                    ins = dve.tensor_tensor(out=c_cw[:, :, :], in0=c_cw[:, :, :], in1=c_rz[:, :].unsqueeze(2).broadcast_to([TILE, NT, NE]), op=ALU.mult)
                ins.then_inc(S["cw"], 1)
                dve.wait_ge(S["out"], 16 * s + 16)
                dve.wait_ge(S["used"], (s + 1) * G + 2)
                alone(dve)
                moe = y_ps[0:TILE, 0:NT * C].rearrange("p (t c) -> p t c", t=NT)
                if layer == 0:
                    dve.wait_ge(S["res"], s + 1)
                    alone(dve)
                    link(dve.tensor_tensor(out=c_x2[:, :, :], in0=c_xr[:, :, :], in1=moe, op=ALU.add))
                    dve.sem_inc(S["x2"], 1)
                    mean_var(c_x2, S["stat2"])
                    dve.wait_ge(S["rstd2"], s + 1)
                    alone(dve)
                    normalise(dve, c_x2, c_mv, c_rs, c_xn, S["norm2"])
                else:
                    dve.tensor_tensor(out=c_x2[:, :, :], in0=c_tok[:, :, :], in1=moe, op=ALU.add).then_inc(S["x2"], 1)
                    
        names = list(w)
        loads = len(names) + 1

        with nc.Block() as block:
            @block.sync
            def _(sp):
                for name in names:
                    sp.dma_start(k[name][:], w[name]).then_inc(w_in, 16)
                sp.wait_ge(w_pool, 1)
                for pad in (vpad_d, cpad_d):
                    for row in (0, PW - 1):
                        sp.dma_start(pad[:, :, row, :].rearrange("b c w -> c b w"), zpad[:]).then_inc(pad_out, 16)
                sp.wait_ge(pad_out, 64)
                for s, start in ahead:
                    sp.sem_inc(s, start)

            @block.gpsimd
            def _(pool):
                pool.memset(zpad[:], 0.0).then_inc(w_pool, 1)
                for i in range(2):
                    pool.memset(a_vT[i][:], 0.0)
                pool.memset(c_xp[:], 0.0)
                for kv in b_kv:
                    pool.memset(kv[:, :, 2 * C:KV1], 1.0)

            @block.vector
            def _(dve):
                for xT in a_xT + [c_xT]:
                    dve.memset(xT[C:C + 1, :], 1.0)
                dve.wait_ge(w_in, 16 * len(names))
                alone(dve)
                for j in range(9):
                    dve.tensor_scalar(out=lepe_tap[:, j, :], in0=k["outT"][:, :], scalar1=k["lepe"][:, j:j + 1], scalar2=None, op0=ALU.mult)
                dve.tensor_scalar(out=conv_tap[:, :, :], in0=k["conv"][:, :, :], scalar1=0.0, scalar2=None, op0=ALU.is_ge).then_inc(w_dve, 1)
                dve.wait_ge(w_dve, 1)
                dve.tensor_scalar(out=conv_tap[:, :, :], in0=conv_tap[:, :, :], scalar1=2.0, scalar2=-1.0, op0=ALU.mult, op1=ALU.add)
                dve.wait_ge(w_pe, 1)
                dve.tensor_tensor(out=out_bias[:, :], in0=a_ps[0:C, 0:1], in1=k["outb"][:, :], op=ALU.add)

            @block.tensor
            def _(pe):
                pe.wait_ge(w_in, 16 * len(names))
                alone(pe)
                pe.matmul(a_ps[0:C, 0:1], k["outT"][:, :], k["lepeb"][:, :], start=True, stop=True).then_inc(w_pe, 1)

        TURNS = NSTRIP // 2
        for sp_f, pe_f, act_f, dve_f, pool_f in ((sp_a, pe_a, act_a, dve_a, pool_a), (sp_t, pe_t, act_t, dve_t, None)):
            with nc.Block() as block:
                @block.sync
                def _(sp):
                    with sp.Fori(0, TURNS) as tau:
                        sp_f(sp, tau)
                    if sp_f is sp_a:
                        for i in range(2):
                            sp.wait_ge(a_out[i], 96 * TURNS + 80)
                            alone(sp)

                @block.tensor
                def _(pe):
                    with pe.Fori(0, TURNS) as tau:
                        pe_f(pe, tau)

                @block.scalar
                def _(act):
                    with act.Fori(0, TURNS) as tau:
                        act_f(act, tau)

                @block.vector
                def _(dve):
                    with dve.Fori(0, TURNS) as tau:
                        dve_f(dve, tau)

                if pool_f is not None:
                    @block.gpsimd
                    def _(pool):
                        with pool.Fori(0, TURNS) as tau:
                            pool_f(pool, tau)

        with nc.Block() as block:
            def turns(eng, f):
                f(eng, 0, first=True)
                with eng.Fori(1, TURNS - 1) as tau:
                    f(eng, tau)
                f(eng, TURNS - 1, last=True)

            @block.sync
            def _(sp):
                turns(sp, sp_b)
                for i in range(2):
                    sp.wait_ge(b_out[i], 16 * TURNS + 16)
                    alone(sp)

            @block.tensor
            def _(pe):
                turns(pe, pe_b)

            @block.scalar
            def _(act):
                turns(act, act_b)

            @block.vector
            def _(dve):
                turns(dve, dve_b)

            @block.gpsimd
            def _(pool):
                turns(pool, pool_b)

        for layer in (0, 1):
            with nc.Block() as block:
                @block.sync
                def _(sp):
                    with sp.Fori(0, TURNS) as tau:
                        sp_c(sp, tau, layer)
                    sp.wait_ge(cs[layer]["out"], 16 * NSTRIP + 16)
                    alone(sp)
                    if layer == 0:
                        sp.wait_ge(cs[layer]["pout"], 16 * NSTRIP + 16)
                        alone(sp)

                @block.tensor
                def _(pe):
                    with pe.Fori(0, TURNS) as tau:
                        pe_c(pe, tau, layer)

                @block.scalar
                def _(act):
                    with act.Fori(0, TURNS) as tau:
                        act_c(act, tau, layer)

                @block.vector
                def _(dve):
                    with dve.Fori(0, TURNS) as tau:
                        dve_c(dve, tau, layer)

                @block.gpsimd
                def _(pool):
                    with pool.Fori(0, TURNS) as tau:
                        pool_c(pool, tau, layer)


def kernel(**inputs):
    import numpy as np
    import concourse.bacc as bacc
    from concourse.bass_utils import run_bass_kernel_spmd as run

    a = {n: np.asarray(v) for n, v in inputs.items()}
    f = np.float32
    lay = {}
    lay["wqkv"] = np.concatenate([a["L0_conv_qkv_w"].T, a["L0_conv_qkv_b"][None, :]])
    lay["outT"] = a["L0_conv_out_w"].T
    lay["outeo"] = a["L0_conv_out_w"].T.reshape(HP, 2, HD, C).transpose(0, 2, 1, 3).reshape(32, 2, C)
    lay["outb"] = a["L0_conv_out_b"].reshape(C, 1)
    lay["lepe"] = a["L0_conv_lepe_w"].reshape(C, 9)
    lay["lepeb"] = a["L0_conv_lepe_b"].reshape(C, 1)
    lay["conv"] = a["L1_conv_kernel"].reshape(9, C, C).transpose(1, 0, 2)
    lay["gate_0"] = np.concatenate([a["L0_ffn_router_w"].T, np.zeros((1, NE), f)])
    lay["gate_1"] = np.concatenate([a["L1_ffn_gate_w"], a["L1_ffn_gate_b"][None, :]])
    lay["w1_0"] = a["L0_ffn_w1"].reshape(4, 2, C, C).transpose(2, 0, 1, 3).reshape(C, 4, 128)
    lay["b1_0"] = a["L0_ffn_b1"].reshape(4, 128).T
    lay["w2_0"] = a["L0_ffn_w2"].reshape(4, 128, C).transpose(1, 0, 2)
    lay["b2_0"] = a["L0_ffn_b2"]
    lay["w1_1"] = a["L1_ffn_W1"].transpose(1, 0, 2)
    lay["b1_1"] = a["L1_ffn_b1"].T
    lay["w2_1"] = a["L1_ffn_W2"].transpose(1, 0, 2)
    lay["b2_1"] = a["L1_ffn_b2"]
    rows = np.arange(128)
    lay["ident"] = np.eye(128, dtype=f)
    lay["head"] = (((rows % C) // HD)[:, None] == np.arange(NHEAD)[None, :]).astype(f) * f(C ** -0.5)
    expert = np.arange(NE)
    lay["sel_0"] = (expert[:, None, None] == 2 * np.arange(4)[None, :, None] + (rows // C)[None, None, :]).astype(f)
    lay["sel_1"] = np.broadcast_to((expert[:, None, None] == expert[None, :, None]), (NE, NE, 128)).astype(f)
    lay["iota"] = np.broadcast_to(expert.astype(f), (128, NE))
    lay["mhalf"] = np.full((128, NT), -0.5, f)

    nc = bacc.Bacc("TRN2", target_bir_lowering=False, num_devices=1)
    arrays = {"in_x": np.ascontiguousarray(a["x"])}
    x = nc.dram_tensor("in_x", a["x"].shape, F32, kind="ExternalInput").ap()
    w = {}
    for name, v in lay.items():
        v = np.ascontiguousarray(v)
        arrays["in_" + name] = v
        w[name] = nc.dram_tensor("in_" + name, v.shape, F32, kind="ExternalInput").ap()
    out = nc.dram_tensor("out_0", (B, H, W, C), F32, kind="ExternalOutput").ap()
    program(nc, x, out, w)
    r = run(nc, [arrays], core_ids=[0])
    return r.results[0]["out_0"]
```

```python
import concourse.bass as bass
from concourse import mybir
from contextlib import ExitStack

F32 = mybir.dt.float32
U32 = mybir.dt.uint32
ALU = mybir.AluOpType
ACT = mybir.ActivationFunctionType
AX = mybir.AxisListType

B, H, W, C = 8, 56, 56, 64
NWIN = 7
REG = NWIN * NWIN
RH = H // NWIN
RTOK = RH * RH
NHEAD, HD, TOPK = 8, 8, 4
NKEY = TOPK * RTOK
KSEL = NKEY // 8
HP = NHEAD // 2
STRIP = RH * W
NSTRIP = B * NWIN
TILE, NT = 112, 4
NE = 8
PW = W + 2
NREG = B * REG
SLOTS = 2 * NWIN
TURNS = NSTRIP // 2
RING = 7
AHEAD = 5
GONE = -3.0e38
KV1 = 2 * C + 1


def program(nc, x, out, w):
    ctx = ExitStack()
    with ctx:
        def sb(name, shape, dt=F32):
            return ctx.enter_context(nc.sbuf_tensor(name, shape, dt))

        def pb(name):
            return ctx.enter_context(nc.psum_tensor(name, [128, 512], F32))

        ahead = []

        def sem(name, start=0):
            s = ctx.enter_context(nc.semaphore(name))
            if start:
                ahead.append((s, start))
            return s

        def sems(name, n, start=0):
            return [sem(f"{name}{k}", start) for k in range(n)]

        def alone(eng):
            eng.sem_inc(passed[eng.engine], 1)

        def split(eng, n, by):
            return (n // by, n % by) if isinstance(n, int) else (eng.snap(n // by), eng.snap(n % by))

        def dram(name, shape, dt=F32):
            return nc.dram_tensor(name, shape, dt).ap()

        q_d = dram("q_d", [NREG, C, RTOK])
        kv_d = dram("kv_d", [NREG, RTOK, 2 * C])
        qr_d = dram("qr_d", [NSTRIP, C, NWIN])
        kr_d = dram("kr_d", [B, C, REG])
        idx_d = dram("idx_d", [NREG, 8], U32)
        vpad_d = dram("vpad_d", [B, C, PW, PW])
        at_d = dram("at_d", [NSTRIP, 32, 2 * STRIP])
        x2_d = dram("x2_d", [NSTRIP, TILE, NT * C])
        cpad_d = dram("cpad_d", [B, C, PW, PW])

        x_s = x.rearrange("b y x c -> (b y x) c").rearrange("(s t p) c -> s p t c", t=NT, p=TILE)
        out_s = out.rearrange("b y x c -> (b y x) c").rearrange("(s t p) c -> s p t c", t=NT, p=TILE)

        k = {name: sb("k_" + name, list(ap.shape)) for name, ap in w.items()}
        lepe_tap = sb("lepe_tap", [C, 9, C])
        conv_tap = sb("conv_tap", [C, 9, C])
        out_bias = sb("out_bias", [C, 1])
        zpad = sb("zpad", [C, B, PW])

        a_x = [sb(f"a_x{i}", [TILE, NT, C]) for i in range(2)]
        a_st = [sb(f"a_st{i}", [TILE, NT, 6]) for i in range(2)]
        a_mv = [sb(f"a_mv{i}", [TILE, NT, 2]) for i in range(2)]
        a_rs = [sb(f"a_rs{i}", [TILE, NT]) for i in range(2)]
        a_xn = [sb(f"a_xn{i}", [TILE, NT, C]) for i in range(2)]
        a_xT = [sb(f"a_xT{i}", [C + 1, STRIP]) for i in range(2)]
        a_qk = [sb(f"a_qk{i}", [128, NWIN, RTOK]) for i in range(2)]
        a_v = [sb(f"a_v{i}", [RTOK, NWIN, C]) for i in range(2)]
        a_vT = [sb(f"a_vT{i}", [C, RH, PW]) for i in range(2)]
        a_sum = [sb(f"a_sum{i}", [128, NWIN]) for i in range(2)]

        t_q = [sb(f"t_q{i}", [C, NWIN]) for i in range(2)]
        t_k = [sb(f"t_k{i}", [C, REG]) for i in range(2)]
        t_a = [sb(f"t_a{i}", [NWIN, REG]) for i in range(2)]
        t_v = [sb(f"t_v{i}", [NWIN, 8]) for i in range(2)]
        t_i = [sb(f"t_i{i}", [NWIN, 8], U32) for i in range(2)]

        b_kv = [sb(f"b_kv{i}", [128, 2, KV1]) for i in range(RING)]
        b_q = [sb(f"b_q{i}", [128, RTOK]) for i in range(RING)]
        b_qe = [sb(f"b_qe{i}", [128, NHEAD, RTOK]) for i in range(2)]
        b_s = [sb(f"b_s{i}", [128, HP, NKEY]) for i in range(2)]
        b_r = [sb(f"b_r{i}", [128, HP, NKEY]) for i in range(2)]
        b_e = [sb(f"b_e{i}", [128, HP, NKEY]) for i in range(2)]
        b_v8 = [sb(f"b_v8{i}", [128, HP, KSEL]) for i in range(2)]
        b_nm = [sb(f"b_nm{i}", [128, HP]) for i in range(2)]
        b_pT = [sb(f"b_pT{i}", [128, 512]) for i in range(2)]
        b_o = sb("b_o", [128, HD + HP * (C + 1 + 2 * HD)])
        b_rec = sb("b_rec", [128, HP])
        b_on = sb("b_on", [128, HP, HD])
        b_at = [sb(f"b_at{i}", [32, 2, RH, W]) for i in range(2)]

        def buffers(n):
            d = dict(
                x=[sb(f"{n}x{i}", [TILE, NT, C]) for i in range(2)],
                win=[sb(f"{n}win{i}", [C, RH + 2, PW]) for i in range(2)],
                h=[sb(f"{n}h{i}", [128, STRIP]) for i in range(2)],
                cb=[sb(f"{n}cb{i}", [128, STRIP]) for i in range(2)],
                m=[sb(f"{n}m{i}", [TILE, NT, NE]) for i in range(2)],
                pi=sb(n + "pi", [TILE, NT, 8], U32))
            for name, shape in (("yT", [C, STRIP]), ("tok", [TILE, NT, C]), ("st", [TILE, NT, 6]), ("mv", [TILE, NT, 2]),
                                ("rs", [TILE, NT]), ("xn", [TILE, NT, C]), ("xr", [TILE, NT, C]), ("xT", [C + 1, STRIP]),
                                ("lm", [TILE, NT]), ("l", [TILE, NT, NE]), ("p", [TILE, NT, NE]), ("z", [TILE, NT]),
                                ("rz", [TILE, NT]), ("pv", [TILE, NT, 8]), ("pf", [TILE, NT, 8]), ("cw", [TILE, NT, NE]),
                                ("cwT", [NE, STRIP]), ("x2", [TILE, NT, C])):
                d[name] = sb(n + name, shape)
            return d

        cb_ = [buffers("c0_"), buffers("c1_")]
        c_at = [sb(f"c_at{i}", [32, 2, STRIP]) for i in range(2)]
        c_xp = sb("c_xp", [C, RH, PW])

        s_ps = [pb("s_ps0"), pb("s_ps1")]
        pT_ps, o_ps, a_ps = pb("pT_ps"), pb("o_ps"), pb("a_ps")
        y_ps, h_ps, g_ps = pb("y_ps"), pb("h_ps"), pb("g_ps")

        passed = {e.engine: ctx.enter_context(nc.semaphore(f"passed_{n}")) for n, e in
                  (("pe", nc.tensor), ("act", nc.scalar), ("dve", nc.vector), ("pool", nc.gpsimd), ("sp", nc.sync))}
        w_in, w_dve, w_pe, w_pool, pad_out = sem("w_in"), sem("w_dve"), sem("w_pe"), sem("w_pool"), sem("pad_out")
        a_in = sems("a_in", 2)
        a_stat = sem("a_stat")
        a_bn = sem("a_bn")
        a_tmp = sem("a_tmp")
        a_rstd = sem("a_rstd")
        a_norm = sem("a_norm", 2)
        a_full = sem("a_full")
        a_ev = sem("a_ev", 8)
        a_pool = sem("a_pool", 2)
        a_out = sems("a_out", 2, 5 * 16)
        t_in = sems("t_in", 2)
        t_full, t_ev, t_max, t_idx = sem("t_full"), sem("t_ev", 2), sem("t_max"), sem("t_idx", 2)
        t_out = sems("t_out", 2, 16)
        b_in = sems("b_in", RING)
        b_qx = sem("b_qx")
        b_qk = sem("b_qk", 2)
        b_sc = sem("b_sc", 1)
        b_chain = sem("b_chain")
        b_sel = sem("b_sel")
        b_neg = sem("b_neg")
        b_exp = sem("b_exp", 2)
        b_msk = sem("b_msk")
        b_prob = sem("b_prob", 2)
        b_pt = sem("b_pt")
        b_ptc = sem("b_ptc", 1)
        b_pv = sem("b_pv", RING)
        b_oc = sem("b_oc")
        b_rc = sem("b_rc")
        b_nrm = sem("b_nrm", 1)
        b_ot = sem("b_ot", 1)
        b_att = sem("b_att", 1)
        b_out = sems("b_out", 2, 16)
        cs = []
        for layer in (0, 1):
            n = f"c{layer}_"
            cs.append(dict(
                x_in=sems(n + "x_in", 2), free=sem(n + "free", 2),
                y=sem(n + "y"), yT=sem(n + "yT"), yt=sem(n + "yt", 1), stat=sem(n + "stat"),
                tmp=sem(n + "tmp"), rstd=sem(n + "rstd"), norm=sem(n + "norm"), res=sem(n + "res"),
                xt=sem(n + "xt"), xT=sem(n + "xT"), lg=sem(n + "lg"), chain=sem(n + "chain"), ls=sem(n + "ls"),
                ex=sem(n + "ex"), cw=sem(n + "cw"), ct=sem(n + "ct"), cT=sem(n + "cT"),
                h=sem(n + "h"), ge=sem(n + "ge", 1), cb=sem(n + "cb", 1), hc=sem(n + "hc"), used=sem(n + "used", 2),
                x2=sem(n + "x2", 1), out=sem(n + "out", 16), pout=sem(n + "pout", 16)))
            cs[-1].update(stat2=sem(n + "stat2"), rstd2=sem(n + "rstd2"), norm2=sem(n + "norm2"),
                          pt=sem(n + "pt"), pT=sem(n + "pT", 1))

        def stats(dve, src, st, mv, chain, chained, then):
            for t in range(NT):
                dve.bn_stats(out=st[:, t, :], in_=src[:, t, :]).then_inc(chain, 1)
            for t in range(NT):
                dve.wait_ge(chain, chained + t + 1)
                alone(dve)
                last = dve.bn_aggr(out=mv[:, t, :], in_=st[:, t, :])
            last.then_inc(then, 1)

        def rstd(pool, mv, rs, eps, tmp, tmped, then):
            pool.tensor_scalar(out=rs[:, :], in0=mv[:, :, 1], scalar1=eps, scalar2=1.0,
                               op0=ALU.add, op1=ALU.mult).then_inc(tmp, 1)
            pool.wait_ge(tmp, tmped + 1)
            pool.tensor_tensor(out=rs[:, :], in0=rs[:, :], in1=k["mhalf"][0:TILE, 0:NT],
                               op=ALU.pow).then_inc(then, 1)

        def normalise(dve, src, mv, rs, dst, chain, count, then):
            wide = [TILE, NT, C]
            dve.tensor_tensor(out=dst[:, :, :], in0=src[:, :, :], in1=mv[:, :, 0:1].broadcast_to(wide),
                              op=ALU.subtract).then_inc(chain, 1)
            dve.wait_ge(chain, count)
            alone(dve)
            dve.tensor_tensor(out=dst[:, :, :], in0=dst[:, :, :], in1=rs[:, :].unsqueeze(2).broadcast_to(wide),
                              op=ALU.mult).then_inc(then, 1)

        def to_channels(pe, src, ps):
            for t in range(NT):
                last = pe.transpose(ps[0:C, t * TILE:(t + 1) * TILE], src[:, t, :], k["ident"][0:TILE, 0:TILE])
            return last


        def sp_a(sp, tau, r):
            i, step = r // NWIN, r % NWIN
            s = tau * 2 + i
            if step == 0:
                sp.wait_ge(a_norm, s + 1)
                sp.dma_start(a_x[i][:], x_s[bass.ds(s, 1)].rearrange("a p t c -> (a p) t c")).then_inc(a_in[i], 16)
            if step == 6:
                b, y = split(sp, s, NWIN)
                put = a_out[i]
                sp.wait_ge(a_pool, s + 3)
                sp.dma_start(q_d[bass.ds(s * NWIN, NWIN)].rearrange("w c t -> c w t"), a_qk[i][0:C]).then_inc(put, 16)
                sp.dma_start(kv_d[bass.ds(s * NWIN, NWIN), :, 0:C].rearrange("w c t -> c w t"),
                             a_qk[i][C:128]).then_inc(put, 16)
                sp.dma_start(qr_d[bass.ds(s, 1)].rearrange("a c w -> (a c) w"), a_sum[i][0:C]).then_inc(put, 16)
                with nc.allow_non_contiguous_dma(reason="seven region sums a row"):
                    sp.dma_start(kr_d[bass.ds(b, 1), :, bass.ds(y * NWIN, NWIN)].rearrange("a c w -> (a c) w"),
                                 a_sum[i][C:128]).then_inc(put, 16)
                sp.wait_ge(a_ev, 4 * s + 12)
                sp.dma_start(kv_d[bass.ds(s * NWIN, NWIN), :, C:2 * C].rearrange("w t c -> t w c"),
                             a_v[i][:]).then_inc(put, 16)
                sp.dma_start(vpad_d[bass.ds(b, 1), :, bass.ds(y * RH + 1, RH), :].rearrange("a c h w -> (a c) h w"),
                             a_vT[i][:]).then_inc(put, 16)

        def dve_a(dve, tau, r):
            i, step = r // NWIN, r % NWIN
            s = tau * 2 + i
            if step == 3:
                dve.wait_ge(a_in[i], 16 * (tau + 1))
                dve.wait_ge(a_norm, s + 1)
                alone(dve)
                stats(dve, a_x[i], a_st[i], a_mv[i], a_bn, 5 * s, a_stat)
            if step == 4:
                dve.wait_ge(a_rstd, s + 1)
                dve.wait_ge(a_ev, 4 * s + 1)
                alone(dve)
                normalise(dve, a_x[i], a_mv[i], a_rs[i], a_xn[i], a_bn, 5 * s + 5, a_norm)
            if step == 6:
                dve.wait_ge(a_ev, 4 * s + 10)
                dve.wait_ge(a_out[i], 96 * tau + 80)
                dve.tensor_reduce(out=a_sum[i][:, :], in_=a_qk[i][:], op=ALU.add, axis=AX.X).then_inc(a_pool, 1)

        def pool_a(pool, tau, r):
            i, step = r // NWIN, r % NWIN
            s = tau * 2 + i
            if step == 3:
                pool.wait_ge(a_stat, s + 1)
                alone(pool)
                rstd(pool, a_mv[i], a_rs[i], 1e-6, a_tmp, s, a_rstd)

        def pe_a(pe, tau, r):
            i, step = r // NWIN, r % NWIN
            s = tau * 2 + i
            if step == 5:
                pe.wait_ge(a_norm, s + 3)
                alone(pe)
                to_channels(pe, a_xn[i], a_ps).then_inc(a_full, 1)
                pe.wait_ge(a_ev, 4 * s + 9)
                alone(pe)
                pe.matmul(a_ps[:, 0:STRIP], k["wqkv"][:, 0:128], a_xT[i][:, :], start=True, stop=True).then_inc(a_full, 1)
            if step == 6:
                pe.wait_ge(a_ev, 4 * s + 10)
                alone(pe)
                for n in range(NWIN):
                    last = pe.matmul(a_ps[0:RTOK, n * C:(n + 1) * C], a_xT[i][:, n * RTOK:(n + 1) * RTOK],
                                     k["wqkv"][:, 128:192], start=True, stop=True)
                last.then_inc(a_full, 1)
                pe.wait_ge(a_ev, 4 * s + 11)
                alone(pe)
                pe.matmul(a_ps[0:C, 0:STRIP], k["wqkv"][:, 128:192],
                          a_xT[i][:, :].rearrange("c (w h q) -> c h w q", w=NWIN, h=RH),
                          start=True, stop=True).then_inc(a_full, 1)
                pe.wait_ge(a_ev, 4 * s + 12)
                alone(pe)

        def act_a(act, tau, r):
            i, step = r // NWIN, r % NWIN
            s = tau * 2 + i
            if step == 5:
                act.wait_ge(a_full, 4 * s + 1)
                act.activation(a_xT[i][0:C, :].rearrange("c (w h q) -> c h w q", w=NWIN, h=RH),
                               a_ps[0:C, 0:STRIP].rearrange("c (h w q) -> c h w q", h=RH, w=NWIN), ACT.Copy).then_inc(a_ev, 1)
                act.wait_ge(a_out[i], 96 * tau + 80)
                act.wait_ge(a_full, 4 * s + 2)
                act.wait_ge(a_pool, s + 1)
                act.activation(a_qk[i][:].rearrange("c w t -> c (w t)"), a_ps[:, 0:STRIP], ACT.Copy).then_inc(a_ev, 1)
            if step == 6:
                act.wait_ge(a_full, 4 * s + 3)
                act.activation(a_v[i][:].rearrange("t w c -> t (w c)"), a_ps[0:RTOK, 0:STRIP], ACT.Copy).then_inc(a_ev, 1)
                act.wait_ge(a_full, 4 * s + 4)
                act.activation(a_vT[i][:, :, 1:W + 1], a_ps[0:C, 0:STRIP].rearrange("c (h w) -> c h w", h=RH),
                               ACT.Copy).then_inc(a_ev, 1)

        def sp_t(sp, tau, r, on):
            i, step = r // NWIN, r % NWIN
            s = tau * 2 + i
            if step == 3:
                b, _ = split(sp, s, NWIN)
                for j in range(2):
                    sp.wait_ge(a_out[j], 96 * (on["a"] if "a" in on else TURNS) + 80)
                    alone(sp)
                sp.wait_ge(t_ev, s + 1)
                sp.dma_start(t_q[i][:], qr_d[bass.ds(s, 1)].rearrange("a c w -> (a c) w")).then_inc(t_in[i], 16)
                sp.dma_start(t_k[i][:], kr_d[bass.ds(b, 1)].rearrange("a c w -> (a c) w")).then_inc(t_in[i], 16)
            if step == 6:
                sp.wait_ge(t_idx, s + 3)
                sp.dma_start(idx_d[bass.ds(s * NWIN, NWIN)], t_i[i][:]).then_inc(t_out[i], 16)

        def pe_t(pe, tau, r):
            i, step = r // NWIN, r % NWIN
            s = tau * 2 + i
            if step == 5:
                pe.wait_ge(t_in[i], 32 * (tau + 1))
                alone(pe)
                pe.matmul(a_ps[0:NWIN, 0:REG], t_q[i][:, :], t_k[i][:, :], start=True, stop=True).then_inc(t_full, 1)
                pe.wait_ge(t_ev, s + 3)
                alone(pe)

        def act_t(act, tau, r):
            i, step = r // NWIN, r % NWIN
            s = tau * 2 + i
            if step == 5:
                act.wait_ge(t_full, s + 1)
                act.wait_ge(t_idx, s + 1)
                act.activation(t_a[i][:, :], a_ps[0:NWIN, 0:REG], ACT.Copy).then_inc(t_ev, 1)

        def dve_t(dve, tau, r):
            i, step = r // NWIN, r % NWIN
            s = tau * 2 + i
            if step == 6:
                dve.wait_ge(t_ev, s + 3)
                alone(dve)
                dve.max(out=t_v[i][:, :], in_=t_a[i][:, :]).then_inc(t_max, 1)
                dve.wait_ge(t_out[i], 16 * tau + 16)
                dve.wait_ge(t_max, s + 1)
                alone(dve)
                dve.max_index(out=t_i[i][:, :], in_max=t_v[i][:, :], in_values=t_a[i][:, :]).then_inc(t_idx, 1)

        def sp_gather(sp, tau, r):
            reg, slot = tau * SLOTS + r, r % RING
            b, _ = split(sp, reg, REG)
            got = b_in[slot]
            if r % NWIN == 0:
                sp.wait_ge(t_out[(r // NWIN) % 2], 16 * (tau + r // SLOTS) + 32)
                alone(sp)
            sp.wait_ge(b_pv, reg + 1)
            alone(sp)
            best = [sp.value_load(idx_d[bass.ds(reg, 1), j:j + 1], min_val=0, max_val=REG - 1) for j in range(TOPK)]
            for j in range(TOPK):
                src = sp.snap(best[j] + b * REG)
                half = (j % 2) * RTOK
                sp.dma_start(b_kv[slot][half:half + RTOK, j // 2, 0:2 * C],
                             kv_d[bass.ds(src, 1)].rearrange("a p c -> (a p) c")).then_inc(got, 16)
            for half in (0, C):
                sp.dma_start(b_q[slot][half:half + C, :], q_d[bass.ds(reg, 1)].rearrange("a c t -> (a c) t")).then_inc(got, 16)

        def pool_spread(pool, tau, r):
            reg = tau * SLOTS + r
            pool.wait_ge(b_in[r % RING], 96 * (tau * 2 + r // RING + 1))
            pool.wait_ge(b_qk, reg + 1)
            pool.tensor_tensor(out=b_qe[r % 2][:, :, :],
                               in0=b_q[r % RING][:, :].unsqueeze(1).broadcast_to([128, NHEAD, RTOK]),
                               in1=k["head"][:, :].unsqueeze(2).broadcast_to([128, NHEAD, RTOK]),
                               op=ALU.mult).then_inc(b_qx, 1)

        def pe_scores(pe, tau, r):
            reg = tau * SLOTS + r
            pe.wait_ge(b_in[r % RING], 96 * (tau * 2 + r // RING + 1))
            pe.wait_ge(b_qx, reg + 1)
            pe.wait_ge(b_sc, reg + 1)
            alone(pe)
            for half in range(2):
                part = slice(half * C, half * C + C)
                for t in range(HP):
                    last = pe.matmul(s_ps[half][:, t * 128:(t + 1) * 128],
                                     b_qe[r % 2][part, 2 * t:2 * t + 2, :].rearrange("c h t -> c (h t)"),
                                     b_kv[r % RING][part, :, 0:RTOK], start=True, stop=True)
            last.then_inc(b_qk, 1)

        def act_scores(act, tau, r):
            reg = tau * SLOTS + r
            act.wait_ge(b_exp, reg + 1)
            act.wait_ge(b_qk, reg + 3)
            for half in range(2):
                last = act.activation(b_s[r % 2][:].rearrange("p t (a h q) -> p h t a q", h=2, q=RTOK)[:, half],
                                      s_ps[half][:, :].rearrange("p (t a q) -> p t a q", t=HP, a=2), ACT.Copy)
            last.then_inc(b_sc, 1)

        def dve_select(dve, tau, r):
            reg, p = tau * SLOTS + r, r % 2
            chain = b_chain
            dve.wait_ge(b_sc, reg + 2)
            dve.wait_ge(b_prob, reg + 1)
            alone(dve)
            rounds = KSEL // 8
            for rnd in range(rounds):
                src = b_s[p] if rnd == 0 else b_r[p]
                for t in range(HP):
                    if rnd:
                        dve.wait_ge(chain, (2 * rnd - 1) * HP + t + 1)
                        alone(dve)
                    dve.max(out=b_v8[p][:, t, 8 * rnd:8 * rnd + 8], in_=src[:, t, :]).then_inc(chain, 1)
                for t in range(HP):
                    dve.wait_ge(chain, 2 * rnd * HP + t + 1)
                    last = dve.match_replace(out=b_r[p][:, t, :], in_to_replace=b_v8[p][:, t, 8 * rnd:8 * rnd + 8],
                                             in_values=src[:, t, :], imm_value=GONE)
                    if rnd < rounds - 1:
                        last.then_inc(chain, 1)
            last.then_inc(b_sel, 1)
            dve.sem_clear(chain)

        def dve_norm(dve, tau, r):
            reg = tau * SLOTS + r
            dve.wait_ge(b_oc, reg + 1)
            alone(dve)
            dve.wait_ge(b_ot, reg + 1)
            alone(dve)
            step = C + 1 + 2 * HD
            sums = b_o[:, 0:HP * (C + 1)].rearrange("p (t c) -> p t c", t=HP)[:, :, C]
            dve.reciprocal(b_rec[:, :], sums).then_inc(b_rc, 1)
            dve.wait_ge(b_rc, reg + 1)
            alone(dve)
            for half in range(2):
                part = slice(half * RTOK, half * RTOK + RTOK)
                own = b_o[part, half * HD:half * HD + HP * step].rearrange("p (t c) -> p t c", c=step)[:, :, 0:HD]
                last = dve.tensor_tensor(out=b_on[part, :, :], in0=own, 
                                         in1=b_rec[part, :].unsqueeze(2).broadcast_to([RTOK, HP, HD]), op=ALU.mult)
            last.then_inc(b_nrm, 1)

        def act_exp(act, tau, r):
            reg, p = tau * SLOTS + r, r % 2
            act.wait_ge(b_sel, reg + 1)
            act.activation(b_nm[p][:, :], b_v8[p][:, :, 0], ACT.Copy, scale=-1.0).then_inc(b_neg, 1)
            act.wait_ge(b_prob, reg + 1)
            act.wait_ge(b_neg, reg + 1)
            for t in range(HP):
                last = act.activation(b_e[p][:, t, :], b_s[p][:, t, :], ACT.Exp, bias=b_nm[p][:, t:t + 1])
            last.then_inc(b_exp, 1)

        def pool_mask(pool, tau, r):
            reg, p = tau * SLOTS + r, r % 2
            pool.wait_ge(b_sel, reg + 1)
            alone(pool)
            pool.tensor_scalar(out=b_r[p][:, :, :], in0=b_r[p][:, :, :], scalar1=GONE, scalar2=None,
                               op0=ALU.is_le).then_inc(b_msk, 1)

        def pool_prob(pool, tau, r):
            reg, p = tau * SLOTS + r, r % 2
            pool.wait_ge(b_msk, reg + 1)
            pool.wait_ge(b_exp, reg + 3)
            pool.tensor_tensor(out=b_e[p][:, :, :], in0=b_e[p][:, :, :], in1=b_r[p][:, :, :],
                               op=ALU.mult).then_inc(b_prob, 1)

        def pe_values(pe, tau, r):
            reg, p = tau * SLOTS + r, r % 2
            pe.wait_ge(b_prob, reg + 3)
            alone(pe)
            for half in range(2):
                pe.wait_ge(b_ptc, 2 * reg + half + 1)
                alone(pe)
                for t in range(2 * half, 2 * half + 2):
                    for c in range(2):
                        col = (t % 2) * 256 + c * 128
                        last = pe.transpose(pT_ps[:, col:col + 128], b_e[p][:, t, c * 128:(c + 1) * 128], k["ident"][:, :])
                last.then_inc(b_pt, 1)
            pe.wait_ge(b_att, reg + 1)
            alone(pe)
            for t in range(HP):
                if t % 2 == 0:
                    pe.wait_ge(b_ptc, 2 * reg + t // 2 + 2)
                    alone(pe)
                for c in range(2):
                    last = pe.matmul(o_ps[:, t * (C + 1):(t + 1) * (C + 1)],
                                     b_pT[t // 2][:, (t % 2) * 256 + c * 128:(t % 2) * 256 + (c + 1) * 128],
                                     b_kv[r % RING][:, c, C:KV1], start=(c == 0), stop=(c == 1))
            last.then_inc(b_pv, 1)

        def act_values(act, tau, r):
            reg = tau * SLOTS + r
            act.wait_ge(b_pv, reg + 7)
            for half in range(2):
                act.wait_ge(b_pt, 2 * reg + half + 1)
                act.activation(b_pT[half][:, :], pT_ps[:, :], ACT.Copy).then_inc(b_ptc, 1)
            act.wait_ge(b_nrm, reg + 1)
            act.wait_ge(b_pv, reg + 8)
            act.activation(b_o[:, 0:HP * (C + 1)], o_ps[:, 0:HP * (C + 1)], ACT.Copy).then_inc(b_oc, 1)

        def pe_out(pe, tau, r):
            reg = tau * SLOTS + r
            pe.wait_ge(b_nrm, reg + 2)
            alone(pe)
            pe.transpose(o_ps[0:32, 0:128], b_on[:, :, :].rearrange("p t c -> p (t c)"), k["ident"][:, :]).then_inc(b_ot, 1)

        def act_out(act, tau, r):
            reg, i, win = tau * SLOTS + r, (r // NWIN) % 2, r % NWIN
            if win == 0:
                act.wait_ge(b_out[i], 16 * tau + 16)
            act.wait_ge(b_ot, reg + 2)
            act.activation(b_at[i][:, :, :, win * RH:(win + 1) * RH],
                           o_ps[0:32, 0:128].rearrange("c (j h q) -> c j h q", j=2, h=RH), ACT.Copy).then_inc(b_att, 1)

        def sp_strip(sp, tau, i):
            s = tau * 2 + i
            sp.wait_ge(b_att, NWIN * (s + 1) + 1)
            sp.dma_start(at_d[bass.ds(s, 1)].rearrange("a c f -> (a c) f"),
                         b_at[i][:].rearrange("c j h w -> c (j h w)")).then_inc(b_out[i], 16)

        groups = (NE // 2, NE)
        w1, w2, b1, b2 = (k["w1_0"], k["w1_1"]), (k["w2_0"], k["w2_1"]), (k["b1_0"], k["b1_1"]), (k["b2_0"], k["b2_1"])
        sel, gate = (k["sel_0"], k["sel_1"]), (k["gate_0"], k["gate_1"])

        def chunk(layer, step):
            return range(0, 4) if step == 4 else range(4, 8) if step == 5 and layer == 1 else range(0)

        def sp_c(sp, tau, r, layer):
            S, D, i, step = cs[layer], cb_[layer], (r // NWIN) % 2, r % NWIN
            s = tau * 2 + r // NWIN
            if step == 0:
                b, y = split(sp, s, NWIN)
                got = S["x_in"][i]
                sp.wait_ge(S["free"], s + 1)
                alone(sp)
                if layer == 0:
                    sp.dma_start(D["x"][i][:], x_s[bass.ds(s, 1)].rearrange("a p t c -> (a p) t c")).then_inc(got, 16)
                    sp.dma_start(D["win"][i][:], vpad_d[bass.ds(b, 1), :, bass.ds(y * RH, RH + 2), :].rearrange("a c h w -> (a c) h w")).then_inc(got, 16)
                    sp.wait_ge(b_out[i], 16 * tau + 32)
                    sp.dma_start(c_at[i][:], at_d[bass.ds(s, 1)].rearrange("a c (j f) -> (a c) j f", j=2)).then_inc(got, 16)
                else:
                    sp.wait_ge(cs[0]["out"], 16 * s + 32)
                    sp.dma_start(D["x"][i][:], x2_d[bass.ds(s, 1)].rearrange("a p (t c) -> (a p) t c", t=NT)).then_inc(got, 16)
                    sp.wait_ge(cs[0]["pout"], 16 * (min(s + 2, 2 * TURNS) if isinstance(s, int) else s + 2) + 16)
                    sp.dma_start(D["win"][i][:], cpad_d[bass.ds(b, 1), :, bass.ds(y * RH, RH + 2), :].rearrange("a c h w -> (a c) h w")).then_inc(got, 16)
            if step == 6:
                b, y = split(sp, s, NWIN)
                sp.wait_ge(S["x2"], s + 2)
                alone(sp)
                if layer == 0:
                    sp.dma_start(x2_d[bass.ds(s, 1)].rearrange("a p (t c) -> (a p) t c", t=NT), D["x2"][:]).then_inc(S["out"], 16)
                    sp.wait_ge(S["pT"], s + 2)
                    sp.dma_start(cpad_d[bass.ds(b, 1), :, bass.ds(y * RH + 1, RH), :].rearrange("a c h w -> (a c) h w"),
                                 c_xp[:]).then_inc(S["pout"], 16)
                else:
                    sp.dma_start(out_s[bass.ds(s, 1)].rearrange("a p t c -> (a p) t c"), D["x2"][:]).then_inc(S["out"], 16)

        def pe_c(pe, tau, r, layer, on):
            S, O, D, G, i, step = cs[layer], cs[1 - layer], cb_[layer], groups[layer], (r // NWIN) % 2, r % NWIN
            s = tau * 2 + r // NWIN
            if step == 0:
                pe.wait_ge(S["x_in"][i], (48, 32)[layer] * (tau + 1))
                alone(pe)
                pe.wait_ge(S["x2"], s + 1)
                alone(pe)
                if layer == 0 and "c1" in on:
                    pe.wait_ge(O["x2"], on["c1"] * 2 + i + 1)
                    alone(pe)
                taps = lepe_tap if layer == 0 else conv_tap
                for j in range(9):
                    last = pe.matmul(y_ps[0:C, 0:STRIP], taps[:, j, :], D["win"][i][:, j // 3:j // 3 + RH, j % 3:j % 3 + W],
                                     start=(j == 0), stop=(j == 8 and layer == 1))
                if layer == 0:
                    for j in range(2):
                        last = pe.matmul(y_ps[0:C, 0:STRIP], k["outeo"][:, j, :], c_at[i][:, j, :], start=False, stop=(j == 1))
                last.then_inc(S["y"], 1)
                pe.wait_ge(S["yT"], s + 1)
                alone(pe)
                if layer == 1 and "c0" in on:
                    pe.wait_ge(O["free"], on["c0"] * 2 + i + 3)
                    alone(pe)
                for t in range(NT):
                    last = pe.transpose(a_ps[0:TILE, t * C:(t + 1) * C], D["yT"][:, t * TILE:(t + 1) * TILE], k["ident"][0:C, 0:C])
                last.then_inc(S["yt"], 1)
            if step == 2:
                pe.wait_ge(S["norm"], s + 1)
                alone(pe)
                if layer == 0:
                    pe.wait_ge(S["pT"], s + 1)
                    alone(pe)
                to_channels(pe, D["xn"], g_ps).then_inc(S["xt"], 1)
                pe.wait_ge(S["xT"], s + 1)
                alone(pe)
                if layer == 0 and "c1" in on:
                    pe.wait_ge(O["free"], on["c1"] * 2 + i + 3)
                    alone(pe)
                if layer == 1 and "c0" in on:
                    pe.wait_ge(O["ls"], on["c0"] * 2 + i + 1)
                    alone(pe)
                for t in range(NT):
                    last = pe.matmul(a_ps[0:TILE, t * NE:(t + 1) * NE], D["xT"][:, t * TILE:(t + 1) * TILE], gate[layer][:, :],
                                     start=True, stop=True)
                last.then_inc(S["lg"], 1)
            if step == 4:
                pe.wait_ge(S["cw"], s + 1)
                alone(pe)
                for t in range(NT):
                    last = pe.transpose(h_ps[0:NE, t * TILE:(t + 1) * TILE], D["cw"][:, t, :], k["ident"][0:TILE, 0:TILE])
                last.then_inc(S["ct"], 1)
                pe.wait_ge(S["cT"], s + 1)
                alone(pe)

            def up(g):
                n = s * G + g
                pe.wait_ge(S["ge"], n + 1)
                alone(pe)
                pe.matmul(h_ps[:, 0:STRIP], w1[layer][:, g, :], D["xT"][0:C, :], start=True, stop=True).then_inc(S["h"], 1)
                pe.wait_ge(S["cb"], n + 1)
                alone(pe)
                pe.matmul(g_ps[:, 0:STRIP], sel[layer][:, g, :], D["cwT"][:, :], start=True, stop=True).then_inc(S["h"], 1)

            todo = chunk(layer, step)
            for g in todo:
                if g == todo[0]:
                    up(g)
                if g == 0:
                    if layer == 1 and "c0" in on:
                        pe.wait_ge(O["x2"], on["c0"] * 2 + i + 2)
                        alone(pe)
                    for t in range(NT):
                        pe.matmul(y_ps[0:TILE, t * C:(t + 1) * C], D["cwT"][:, t * TILE:(t + 1) * TILE], b2[layer][:, :],
                                  start=(t == 0), stop=False, skip_group_check=True)
                if g + 1 in todo:
                    up(g + 1)
                pe.wait_ge(S["hc"], s * G + g + 1)
                alone(pe)
                for t in range(NT):
                    last = pe.matmul(y_ps[0:TILE, t * C:(t + 1) * C], D["h"][g % 2][:, t * TILE:(t + 1) * TILE],
                                     w2[layer][:, g, :], start=False, stop=(g == G - 1), skip_group_check=True)
                last.then_inc(S["used"], 1)
            if step == 6 and layer == 0:
                pe.wait_ge(S["norm2"], s + 1)
                alone(pe)
                to_channels(pe, D["xn"], g_ps).then_inc(S["pt"], 1)

        def act_c(act, tau, r, layer):
            S, D, G, step = cs[layer], cb_[layer], groups[layer], r % NWIN
            s = tau * 2 + r // NWIN
            if step == 0:
                act.wait_ge(S["y"], s + 1)
                act.wait_ge(S["yt"], s + 1)
                if layer == 0:
                    act.activation(D["yT"][:, :], y_ps[0:C, 0:STRIP], ACT.Identity, bias=out_bias[:, 0:1]).then_inc(S["yT"], 1)
                else:
                    act.activation(D["yT"][:, :], y_ps[0:C, 0:STRIP], ACT.Copy).then_inc(S["yT"], 1)
            if step == 2:
                act.wait_ge(S["xt"], s + 1)
                act.activation(D["xT"][0:C, :], g_ps[0:C, 0:STRIP], ACT.Copy).then_inc(S["xT"], 1)
            if step == 3:
                act.wait_ge(S["ls"], s + 1)
                act.activation(D["p"][:, :, :], D["l"][:, :, :], ACT.Exp).then_inc(S["ex"], 1)
            if step == 4:
                act.wait_ge(S["ct"], s + 1)
                act.activation(D["cwT"][:, :], h_ps[0:NE, 0:STRIP], ACT.Copy).then_inc(S["cT"], 1)
            for g in chunk(layer, step):
                n = s * G + g
                act.wait_ge(S["used"], n + 1)
                act.wait_ge(S["h"], 2 * n + 1)
                act.activation(D["h"][g % 2][:, :], h_ps[:, 0:STRIP], ACT.Gelu, bias=b1[layer][:, g:g + 1]).then_inc(S["ge"], 1)
                act.wait_ge(S["h"], 2 * n + 2)
                act.activation(D["cb"][g % 2][:, :], g_ps[:, 0:STRIP], ACT.Copy).then_inc(S["cb"], 1)
            if step == 6 and layer == 0:
                act.wait_ge(S["pt"], s + 1)
                act.wait_ge(S["pout"], 16 * s + 16)
                act.activation(c_xp[:, :, 1:W + 1], g_ps[0:C, 0:STRIP].rearrange("c (h w) -> c h w", h=RH),
                               ACT.Copy).then_inc(S["pT"], 1)

        def pool_c(pool, tau, r, layer):
            S, D, G, step = cs[layer], cb_[layer], groups[layer], r % NWIN
            s = tau * 2 + r // NWIN
            if step == 1:
                pool.wait_ge(S["stat"], s + 1)
                alone(pool)
                rstd(pool, D["mv"], D["rs"], 1e-5, S["tmp"], (2 - layer) * s, S["rstd"])
            if step == 2 and layer == 0:
                pool.wait_ge(S["norm"], s + 1)
                pool.tensor_tensor(out=D["xr"][:, :, :], in0=D["tok"][:, :, :], in1=D["xn"][:, :, :], op=ALU.add).then_inc(S["res"], 1)
            for g in chunk(layer, step):
                pool.wait_ge(S["cb"], s * G + g + 2)
                pool.tensor_tensor(out=D["h"][g % 2][:, :], in0=D["h"][g % 2][:, :], in1=D["cb"][g % 2][:, :],
                                   op=ALU.mult).then_inc(S["hc"], 1)
            if step == 5 and layer == 0:
                pool.wait_ge(S["stat2"], s + 1)
                alone(pool)
                rstd(pool, D["mv"], D["rs"], 1e-6, S["tmp"], 2 * s + 1, S["rstd2"])

        def dve_c(dve, tau, r, layer):
            S, D, G, i, step = cs[layer], cb_[layer], groups[layer], (r // NWIN) % 2, r % NWIN
            s = tau * 2 + r // NWIN
            tok, xn, x2, mv, st, p, cw, m = D["tok"], D["xn"], D["x2"], D["mv"], D["st"], D["p"], D["cw"], D["m"]
            by_expert = [TILE, NT, NE]
            count = [0]

            def link(ins):
                count[0] += 1
                ins.then_inc(S["chain"], 1)
                dve.wait_ge(S["chain"], count[0])

            def mean_var(src, then):
                for t in range(NT):
                    ins = dve.bn_stats(out=st[:, t, :], in_=src[:, t, :])
                    if t < NT - 1:
                        ins.then_inc(S["chain"], 1)
                        count[0] += 1
                link(ins)
                for t in range(NT):
                    ins = dve.bn_aggr(out=mv[:, t, :], in_=st[:, t, :])
                ins.then_inc(then, 1)

            dve.sem_clear(S["chain"])
            if step == 1:
                dve.wait_ge(S["x_in"][i], (48, 32)[layer] * (tau + 1))
                dve.wait_ge(S["yt"], s + 2)
                alone(dve)
                link(dve.tensor_tensor(out=tok[:, :, :], in0=D["x"][i][:, :, :],
                                       in1=a_ps[0:TILE, 0:NT * C].rearrange("p (t c) -> p t c", t=NT), op=ALU.add))
                dve.sem_inc(S["free"], 1)
                mean_var(tok, S["stat"])
            if step == 2:
                dve.wait_ge(S["rstd"], s + 1)
                alone(dve)
                normalise(dve, tok, mv, D["rs"], xn, S["chain"], 1, S["norm"])
            if step == 3:
                dve.wait_ge(S["lg"], s + 1)
                alone(dve)
                lg = a_ps[0:TILE, 0:NT * NE].rearrange("p (t e) -> p t e", t=NT)
                link(dve.tensor_reduce(out=D["lm"][:, :], in_=lg, op=ALU.max, axis=AX.X))
                dve.tensor_tensor(out=D["l"][:, :, :], in0=lg, in1=D["lm"][:, :].unsqueeze(2).broadcast_to(by_expert),
                                  op=ALU.subtract).then_inc(S["ls"], 1)
            if step == 4:
                dve.wait_ge(S["ex"], s + 1)
                alone(dve)
                link(dve.tensor_reduce(out=D["z"][:, :], in_=p[:, :, :], op=ALU.add, axis=AX.X))
                link(dve.reciprocal(D["rz"][:, :], D["z"][:, :]))
                link(dve.tensor_tensor(out=p[:, :, :], in0=p[:, :, :], in1=D["rz"][:, :].unsqueeze(2).broadcast_to(by_expert), op=ALU.mult))
                for t in range(NT):
                    ins = dve.max(out=D["pv"][:, t, :], in_=p[:, t, :])
                link(ins)
                for t in range(NT):
                    ins = dve.max_index(out=D["pi"][:, t, :], in_max=D["pv"][:, t, :], in_values=p[:, t, :])
                link(ins)
                link(dve.tensor_copy(D["pf"][:, :, :], D["pi"][:, :, :]))
                for j in range(2):
                    ins = dve.tensor_tensor(out=m[j][:, :, :], in0=k["iota"][0:TILE, :].unsqueeze(1).broadcast_to(by_expert),
                                            in1=D["pf"][:, :, j:j + 1].broadcast_to(by_expert), op=ALU.is_equal)
                link(ins)
                link(dve.tensor_tensor(out=m[0][:, :, :], in0=m[0][:, :, :], in1=m[1][:, :, :], op=ALU.add))
                ins = dve.tensor_tensor(out=cw[:, :, :], in0=m[0][:, :, :], in1=p[:, :, :], op=ALU.mult)
                if layer == 0:
                    link(ins)
                    link(dve.tensor_tensor(out=D["z"][:, :], in0=D["pv"][:, :, 0], in1=D["pv"][:, :, 1], op=ALU.add))
                    link(dve.tensor_scalar(out=D["z"][:, :], in0=D["z"][:, :], scalar1=1e-12, scalar2=None, op0=ALU.max))
                    link(dve.reciprocal(D["rz"][:, :], D["z"][:, :]))
                    ins = dve.tensor_tensor(out=cw[:, :, :], in0=cw[:, :, :], in1=D["rz"][:, :].unsqueeze(2).broadcast_to(by_expert), op=ALU.mult)
                ins.then_inc(S["cw"], 1)
            if (layer, step) in ((0, 5), (1, 6)):
                dve.wait_ge(S["out"], 16 * s + 16)
                dve.wait_ge(S["used"], (s + 1) * G + 2)
                alone(dve)
                moe = y_ps[0:TILE, 0:NT * C].rearrange("p (t c) -> p t c", t=NT)
                if layer == 0:
                    dve.wait_ge(S["res"], s + 1)
                    alone(dve)
                    link(dve.tensor_tensor(out=x2[:, :, :], in0=D["xr"][:, :, :], in1=moe, op=ALU.add))
                    dve.sem_inc(S["x2"], 1)
                    mean_var(x2, S["stat2"])
                else:
                    dve.tensor_tensor(out=x2[:, :, :], in0=tok[:, :, :], in1=moe, op=ALU.add).then_inc(S["x2"], 1)
            if step == 6 and layer == 0:
                dve.wait_ge(S["rstd2"], s + 1)
                alone(dve)
                normalise(dve, x2, mv, D["rs"], xn, S["chain"], 1, S["norm2"])

        LAG = dict(a=0, t=4, b=5, c0=6, c1=7)
        END = TURNS + LAG["c1"]

        def run(eng, slot):
            marks = sorted({n + e for n in LAG.values() for e in (0, TURNS)} |
                           {LAG["b"] + 1, LAG["b"] + TURNS - 1, LAG["c1"] + 1, END - 1})
            for lo, hi in zip(marks, marks[1:]):
                def segment(n):
                    on = {name: n - lag for name, lag in LAG.items() if lag <= lo < lag + TURNS}
                    first = {name for name, lag in LAG.items() if lo == lag}
                    last = {name for name, lag in LAG.items() if lo == lag + TURNS - 1}
                    slot(on, first, last)
                if hi - lo == 1:
                    segment(lo)
                else:
                    with eng.Fori(lo, hi) as n:
                        segment(n)

        names = list(w)
        with nc.Block() as block:
            @block.sync
            def _(sp):
                for name in names:
                    sp.dma_start(k[name][:], w[name]).then_inc(w_in, 16)
                sp.wait_ge(w_pool, 1)
                for pad in (vpad_d, cpad_d):
                    for row in (0, PW - 1):
                        sp.dma_start(pad[:, :, row, :].rearrange("b c w -> c b w"), zpad[:]).then_inc(pad_out, 16)
                sp.wait_ge(pad_out, 64)
                for s, start in ahead:
                    sp.sem_inc(s, start)

            @block.gpsimd
            def _(pool):
                pool.memset(zpad[:], 0.0).then_inc(w_pool, 1)
                for i in range(2):
                    pool.memset(a_vT[i][:], 0.0)
                pool.memset(c_xp[:], 0.0)
                for kv in b_kv:
                    pool.memset(kv[:, :, 2 * C:KV1], 1.0)

            @block.vector
            def _(dve):
                for xT in a_xT + [cb_[0]["xT"], cb_[1]["xT"]]:
                    dve.memset(xT[C:C + 1, :], 1.0)
                dve.wait_ge(w_in, 16 * len(names))
                alone(dve)
                for j in range(9):
                    dve.tensor_scalar(out=lepe_tap[:, j, :], in0=k["outT"][:, :], scalar1=k["lepe"][:, j:j + 1], scalar2=None, op0=ALU.mult)
                dve.tensor_scalar(out=conv_tap[:, :, :], in0=k["conv"][:, :, :], scalar1=0.0, scalar2=None, op0=ALU.is_ge).then_inc(w_dve, 1)
                dve.wait_ge(w_dve, 1)
                dve.tensor_scalar(out=conv_tap[:, :, :], in0=conv_tap[:, :, :], scalar1=2.0, scalar2=-1.0, op0=ALU.mult, op1=ALU.add)
                dve.wait_ge(w_pe, 1)
                dve.tensor_tensor(out=out_bias[:, :], in0=a_ps[0:C, 0:1], in1=k["outb"][:, :], op=ALU.add)

            @block.tensor
            def _(pe):
                pe.wait_ge(w_in, 16 * len(names))
                alone(pe)
                pe.matmul(a_ps[0:C, 0:1], k["outT"][:, :], k["lepeb"][:, :], start=True, stop=True).then_inc(w_pe, 1)

        with nc.Block() as block:
            @block.sync
            def _(sp):
                def slots(on, first, last):
                    if "b" in first:
                        for r in range(AHEAD):
                            sp_gather(sp, on["b"], r)
                    for r in range(SLOTS):
                        if "b" in on:
                            if r + AHEAD < SLOTS or "b" not in last:
                                sp_gather(sp, on["b"], r + AHEAD)
                            if r == 2 and "b" not in first:
                                sp_strip(sp, on["b"] - 1, 1)
                            if r == NWIN + 2:
                                sp_strip(sp, on["b"], 0)
                        if "c1" in on and (r or "c1" not in first):
                            sp_c(sp, on["c1"], r - 1, 1)
                        if "c0" in on:
                            sp_c(sp, on["c0"], r, 0)
                        if "t" in on:
                            sp_t(sp, on["t"], r, on)
                        if "a" in on:
                            sp_a(sp, on["a"], r)
                    if "b" in last:
                        sp_strip(sp, on["b"], 1)
                    if "c1" in last:
                        sp_c(sp, on["c1"], SLOTS - 1, 1)
                run(sp, slots)
                sp.wait_ge(cs[1]["out"], 16 * 2 * TURNS + 16)
                alone(sp)
                sp.wait_ge(cs[0]["out"], 16 * 2 * TURNS + 16)
                alone(sp)
                sp.wait_ge(cs[0]["pout"], 16 * 2 * TURNS + 16)
                alone(sp)
                for i in range(2):
                    sp.wait_ge(t_out[i], 16 * TURNS + 16)
                    alone(sp)
                    sp.wait_ge(b_out[i], 16 * TURNS + 16)
                    alone(sp)

            @block.tensor
            def _(pe):
                def slots(on, first, last):
                    if "b" in first:
                        pe_scores(pe, on["b"], 0)
                        pe_scores(pe, on["b"], 1)
                    for r in range(SLOTS):
                        if "b" in on:
                            if r + 2 < SLOTS or "b" not in last:
                                pe_scores(pe, on["b"], r + 2)
                            if r >= 2 or "b" not in first:
                                pe_out(pe, on["b"], r - 2)
                            if r >= 1 or "b" not in first:
                                pe_values(pe, on["b"], r - 1)
                        if "c1" in on and (r or "c1" not in first):
                            pe_c(pe, on["c1"], r - 1, 1, on)
                        if "c0" in on:
                            pe_c(pe, on["c0"], r, 0, on)
                        if "t" in on:
                            pe_t(pe, on["t"], r)
                        if "a" in on:
                            pe_a(pe, on["a"], r)
                    if "b" in last:
                        pe_out(pe, on["b"], SLOTS - 2)
                        pe_values(pe, on["b"], SLOTS - 1)
                        pe_out(pe, on["b"], SLOTS - 1)
                    if "c0" in last:
                        pe.wait_ge(cs[0]["pT"], 2 * TURNS + 1)
                        alone(pe)
                run(pe, slots)

            @block.scalar
            def _(act):
                def slots(on, first, last):
                    if "b" in first:
                        act_scores(act, on["b"], 0)
                        act_scores(act, on["b"], 1)
                    for r in range(SLOTS):
                        if "b" in on:
                            act_exp(act, on["b"], r)
                            if r + 2 < SLOTS or "b" not in last:
                                act_scores(act, on["b"], r + 2)
                            if r >= 2 or "b" not in first:
                                act_out(act, on["b"], r - 2)
                            if r >= 1 or "b" not in first:
                                act_values(act, on["b"], r - 1)
                        if "c1" in on and (r or "c1" not in first):
                            act_c(act, on["c1"], r - 1, 1)
                        if "c0" in on:
                            act_c(act, on["c0"], r, 0)
                        if "t" in on:
                            act_t(act, on["t"], r)
                        if "a" in on:
                            act_a(act, on["a"], r)
                    if "b" in last:
                        act_out(act, on["b"], SLOTS - 2)
                        act_values(act, on["b"], SLOTS - 1)
                        act_out(act, on["b"], SLOTS - 1)
                run(act, slots)

            @block.vector
            def _(dve):
                def slots(on, first, last):
                    for r in range(SLOTS):
                        if "b" in on:
                            dve_select(dve, on["b"], r)
                            if r >= 2 or "b" not in first:
                                dve_norm(dve, on["b"], r - 2)
                        if "c1" in on and (r or "c1" not in first):
                            dve_c(dve, on["c1"], r - 1, 1)
                        if "c0" in on:
                            dve_c(dve, on["c0"], r, 0)
                        if "t" in on:
                            dve_t(dve, on["t"], r)
                        if "a" in on:
                            dve_a(dve, on["a"], r)
                    if "b" in last:
                        dve_norm(dve, on["b"], SLOTS - 2)
                        dve_norm(dve, on["b"], SLOTS - 1)
                    if "c1" in last:
                        dve_c(dve, on["c1"], SLOTS - 1, 1)
                run(dve, slots)

            @block.gpsimd
            def _(pool):
                def slots(on, first, last):
                    if "b" in first:
                        for r in range(3):
                            pool_spread(pool, on["b"], r)
                    for r in range(SLOTS):
                        if "b" in on:
                            pool_mask(pool, on["b"], r)
                            if r + 3 < SLOTS or "b" not in last:
                                pool_spread(pool, on["b"], r + 3)
                            pool_prob(pool, on["b"], r)
                        if "c0" in on:
                            pool_c(pool, on["c0"], r, 0)
                        if "c1" in on and (r or "c1" not in first):
                            pool_c(pool, on["c1"], r - 1, 1)
                        if "a" in on:
                            pool_a(pool, on["a"], r)
                run(pool, slots)


def kernel(**inputs):
    import numpy as np
    import concourse.bacc as bacc
    from concourse.bass_utils import run_bass_kernel_spmd as run

    a = {n: np.asarray(v) for n, v in inputs.items()}
    f = np.float32
    lay = {}
    lay["wqkv"] = np.concatenate([a["L0_conv_qkv_w"].T, a["L0_conv_qkv_b"][None, :]])
    lay["outT"] = a["L0_conv_out_w"].T
    lay["outeo"] = a["L0_conv_out_w"].T.reshape(HP, 2, HD, C).transpose(0, 2, 1, 3).reshape(32, 2, C)
    lay["outb"] = a["L0_conv_out_b"].reshape(C, 1)
    lay["lepe"] = a["L0_conv_lepe_w"].reshape(C, 9)
    lay["lepeb"] = a["L0_conv_lepe_b"].reshape(C, 1)
    lay["conv"] = a["L1_conv_kernel"].reshape(9, C, C).transpose(1, 0, 2)
    lay["gate_0"] = np.concatenate([a["L0_ffn_router_w"].T, np.zeros((1, NE), f)])
    lay["gate_1"] = np.concatenate([a["L1_ffn_gate_w"], a["L1_ffn_gate_b"][None, :]])
    lay["w1_0"] = a["L0_ffn_w1"].reshape(4, 2, C, C).transpose(2, 0, 1, 3).reshape(C, 4, 128)
    lay["b1_0"] = a["L0_ffn_b1"].reshape(4, 128).T
    lay["w2_0"] = a["L0_ffn_w2"].reshape(4, 128, C).transpose(1, 0, 2)
    lay["b2_0"] = a["L0_ffn_b2"]
    lay["w1_1"] = a["L1_ffn_W1"].transpose(1, 0, 2)
    lay["b1_1"] = a["L1_ffn_b1"].T
    lay["w2_1"] = a["L1_ffn_W2"].transpose(1, 0, 2)
    lay["b2_1"] = a["L1_ffn_b2"]
    rows = np.arange(128)
    lay["ident"] = np.eye(128, dtype=f)
    lay["head"] = (((rows % C) // HD)[:, None] == np.arange(NHEAD)[None, :]).astype(f) * f(C ** -0.5)
    expert = np.arange(NE)
    lay["sel_0"] = (expert[:, None, None] == 2 * np.arange(4)[None, :, None] + (rows // C)[None, None, :]).astype(f)
    lay["sel_1"] = np.broadcast_to((expert[:, None, None] == expert[None, :, None]), (NE, NE, 128)).astype(f)
    lay["iota"] = np.broadcast_to(expert.astype(f), (128, NE))
    lay["mhalf"] = np.full((128, NT), -0.5, f)

    nc = bacc.Bacc("TRN2", target_bir_lowering=False, num_devices=1)
    arrays = {"in_x": np.ascontiguousarray(a["x"])}
    x = nc.dram_tensor("in_x", a["x"].shape, F32, kind="ExternalInput").ap()
    w = {}
    for name, v in lay.items():
        v = np.ascontiguousarray(v)
        arrays["in_" + name] = v
        w[name] = nc.dram_tensor("in_" + name, v.shape, F32, kind="ExternalInput").ap()
    out = nc.dram_tensor("out_0", (B, H, W, C), F32, kind="ExternalOutput").ap()
    program(nc, x, out, w)
    r = run(nc, [arrays], core_ids=[0])
    return r.results[0]["out_0"]
```

```python
import concourse.bass as bass
from concourse import mybir
from contextlib import ExitStack

F32 = mybir.dt.float32
U32 = mybir.dt.uint32
BF16 = mybir.dt.bfloat16
ALU = mybir.AluOpType
ACT = mybir.ActivationFunctionType
AX = mybir.AxisListType

B, H, W, C = 8, 56, 56, 64
NWIN = 7
REG = NWIN * NWIN
RH = H // NWIN
RTOK = RH * RH
NHEAD, HD, TOPK = 8, 8, 4
NKEY = TOPK * RTOK
KSEL = NKEY // 8
HP = NHEAD // 2
STRIP = RH * W
NSTRIP = B * NWIN
TILE, NT = 112, 4
NE = 8
PW = W + 2
NREG = B * REG
SLOTS = 2 * NWIN
TURNS = NSTRIP // 2
RING = 7
AHEAD = 5
GONE = -3.0e38
VH = 2 * HD + 1
KV = C + HP * VH


def program(nc, x, out, w):
    ctx = ExitStack()
    with ctx:
        def sb(name, shape, dt=F32):
            return ctx.enter_context(nc.sbuf_tensor(name, shape, dt))

        def pb(name):
            return ctx.enter_context(nc.psum_tensor(name, [128, 512], F32))

        ahead = []

        def sem(name, start=0):
            s = ctx.enter_context(nc.semaphore(name))
            if start:
                ahead.append((s, start))
            return s

        def sems(name, n, start=0):
            return [sem(f"{name}{k}", start) for k in range(n)]

        def alone(eng):
            eng.sem_inc(passed[eng.engine], 1)

        def split(eng, n, by):
            return (n // by, n % by) if isinstance(n, int) else (eng.snap(n // by), eng.snap(n % by))

        def dram(name, shape, dt=F32):
            return nc.dram_tensor(name, shape, dt).ap()

        q_d = dram("q_d", [NREG, C, RTOK])
        kv_d = dram("kv_d", [NREG, RTOK, KV])
        qr_d = dram("qr_d", [NSTRIP, C, NWIN])
        kr_d = dram("kr_d", [B, C, REG])
        idx_d = dram("idx_d", [NREG, 8], U32)
        vpad_d = dram("vpad_d", [B, C, PW, PW])
        at_d = dram("at_d", [NSTRIP, 2, 32, STRIP])
        x2_d = dram("x2_d", [NSTRIP, TILE, NT * C])
        cpad_d = dram("cpad_d", [B, 3 * C, PW, PW], BF16)

        x_s = x.rearrange("b y x c -> (b y x) c").rearrange("(s t p) c -> s p t c", t=NT, p=TILE)
        out_s = out.rearrange("b y x c -> (b y x) c").rearrange("(s t p) c -> s p t c", t=NT, p=TILE)

        k = {name: sb("k_" + name, list(ap.shape)) for name, ap in w.items()}
        lepe_tap = sb("lepe_tap", [128, 5, C])
        conv_tap = sb("conv_tap", [128, 9, C], BF16)
        conv_low = sb("conv_low", [128, 6, C], BF16)
        out_bias = sb("out_bias", [C, 1])
        zpad = sb("zpad", [C, B, PW])
        zpadb = sb("zpadb", [C, B, PW], BF16)
        ident_b = sb("ident_b", [128, 128], BF16)
        sel_b = [sb(f"sel_b{n}", [128, g, 128], BF16) for n, g in ((0, NE // 2), (1, NE))]
        b2_b = [sb(f"b2_b{n}", [128, 3, C], BF16) for n in (0, 1)]
        b2_d = [sb(f"b2_d{n}", [128, C]) for n in (0, 1)]

        a_x = [sb(f"a_x{i}", [TILE, NT, C]) for i in range(2)]
        a_st = [sb(f"a_st{i}", [TILE, NT, 6]) for i in range(2)]
        a_mv = [sb(f"a_mv{i}", [TILE, NT, 2]) for i in range(2)]
        a_rs = [sb(f"a_rs{i}", [TILE, NT]) for i in range(2)]
        a_xn = [sb(f"a_xn{i}", [TILE, NT, C]) for i in range(2)]
        a_xT = [sb(f"a_xT{i}", [128, STRIP]) for i in range(2)]
        a_qk = [sb(f"a_qk{i}", [128, NWIN, RTOK]) for i in range(2)]
        a_v = [sb(f"a_v{i}", [RTOK, NWIN, HP, VH]) for i in range(2)]
        a_vT = [sb(f"a_vT{i}", [C, RH, PW]) for i in range(2)]
        a_sum = [sb(f"a_sum{i}", [128, NWIN]) for i in range(2)]

        t_q = [sb(f"t_q{i}", [C, NWIN]) for i in range(2)]
        t_k = [sb(f"t_k{i}", [C, REG]) for i in range(2)]
        t_a = [sb(f"t_a{i}", [NWIN, REG]) for i in range(2)]
        t_v = [sb(f"t_v{i}", [NWIN, 8]) for i in range(2)]
        t_i = [sb(f"t_i{i}", [NWIN, 8], U32) for i in range(2)]

        b_kv = [sb(f"b_kv{i}", [128, 2, KV]) for i in range(RING)]
        b_q = [sb(f"b_q{i}", [128, RTOK]) for i in range(RING)]
        b_qe = [sb(f"b_qe{i}", [128, 2 * NHEAD, RTOK]) for i in range(2)]
        b_s = [sb(f"b_s{i}", [128, HP, NKEY]) for i in range(2)]
        b_r = [sb(f"b_r{i}", [128, HP, NKEY]) for i in range(2)]
        b_e = [sb(f"b_e{i}", [128, HP, NKEY]) for i in range(2)]
        b_v8 = [sb(f"b_v8{i}", [128, HP, KSEL]) for i in range(2)]
        b_nm = [sb(f"b_nm{i}", [128, HP]) for i in range(2)]
        b_pT = [sb(f"b_pT{i}", [128, 512]) for i in range(2)]
        b_o = [sb(f"b_o{i}", [128, HP, VH]) for i in range(2)]
        b_rec = sb("b_rec", [128, HP])
        b_on = sb("b_on", [128, HP, HD])
        b_at = [sb(f"b_at{i}", [32, 2, RH, W]) for i in range(2)]

        def buffers(n):
            d = dict(
                x=[sb(f"{n}x{i}", [TILE, NT, C]) for i in range(2)],
                tok=[sb(f"{n}tok{i}", [TILE, NT, C]) for i in range(2)],
                xr=[sb(f"{n}xr{i}", [TILE, NT, C]) for i in range(2)],
                h=[sb(f"{n}h{i}", [128, STRIP]) for i in range(2)],
                cb=[sb(f"{n}cb{i}", [128, STRIP]) for i in range(2)],
                m=[sb(f"{n}m{i}", [TILE, NT, NE]) for i in range(2)],
                pi=sb(n + "pi", [TILE, NT, 8], U32))
            for name, shape in (("yT", [C, STRIP]), ("pr", [TILE, NT, C]), ("lg", [TILE, NT, NE]), ("xm", [TILE, NT, C]), ("st", [TILE, NT, 6]), ("mv", [TILE, NT, 2]),
                                ("rs", [TILE, NT]), ("mv2", [TILE, NT, 2]), ("rs2", [TILE, NT]), ("xn", [TILE, NT, C]), ("xT", [128, STRIP]),
                                ("lm", [TILE, NT]), ("l", [TILE, NT, NE]), ("p", [TILE, NT, NE]), ("z", [TILE, NT]),
                                ("rz", [TILE, NT]), ("pv", [TILE, NT, 8]), ("pf", [TILE, NT, 8]), ("cw", [TILE, NT, NE]),
                                ("cwd", [TILE, NT, NE]), ("x2", [TILE, NT, C])):
                d[name] = sb(n + name, shape)
            d["cw3"] = sb(n + "cw3", [TILE, NT, 3, NE], BF16)
            d["cwT"] = sb(n + "cwT", [128, STRIP], BF16)
            return d

        cb_ = [buffers("c0_"), buffers("c1_")]
        c_win = [sb(f"c_win{i}", [128, RH + 2, PW]) for i in range(2)]
        c_row = [sb(f"c_row{i}", [128, RH, PW]) for i in range(2)]
        c_cor = [sb(f"c_cor{i}", [128, RH, W]) for i in range(2)]
        c_hm = [sb(f"c_hm{i}", [128, RH + 2, PW], BF16) for i in range(2)]
        c_lo = [sb(f"c_lo{i}", [128, RH + 2, PW], BF16) for i in range(2)]
        c_x3 = sb("c_x3", [TILE, NT, 3, C], BF16)
        c_xd = sb("c_xd", [TILE, NT, C])
        c_hmp = sb("c_hmp", [128, RH, PW], BF16)
        c_lop = sb("c_lop", [C, RH, PW], BF16)

        s_ps = [pb("s_ps0"), pb("s_ps1")]
        pT_ps, o_ps, a_ps = pb("pT_ps"), pb("o_ps"), pb("a_ps")
        y_ps, h_ps, g_ps = pb("y_ps"), pb("h_ps"), pb("g_ps")

        passed = {e.engine: ctx.enter_context(nc.semaphore(f"passed_{n}")) for n, e in
                  (("pe", nc.tensor), ("act", nc.scalar), ("dve", nc.vector), ("pool", nc.gpsimd), ("sp", nc.sync))}
        w_in, w_dve, w_pe, w_pool, pad_out = sem("w_in"), sem("w_dve"), sem("w_pe"), sem("w_pool"), sem("pad_out")
        a_in = sems("a_in", 2)
        a_stat = sem("a_stat")
        a_bn = sem("a_bn")
        a_sub = sem("a_sub")
        a_tmp = sem("a_tmp")
        a_rstd = sem("a_rstd")
        a_norm = sem("a_norm", 2)
        a_full = sem("a_full")
        a_ev = sem("a_ev", 8)
        a_pool = sem("a_pool", 2)
        a_out = sems("a_out", 2, 5 * 16)
        t_in = sems("t_in", 2)
        t_full, t_ev, t_max, t_idx = sem("t_full"), sem("t_ev", 2), sem("t_max"), sem("t_idx", 2)
        t_out = sems("t_out", 2, 16)
        b_in = sems("b_in", RING)
        b_qx = sem("b_qx")
        b_qk = sem("b_qk", 2)
        b_sc = sem("b_sc", 1)
        b_chain = sem("b_chain")
        b_sel = sem("b_sel")
        b_neg = sem("b_neg")
        b_exp = sem("b_exp", 2)
        b_msk = sem("b_msk")
        b_prob = sem("b_prob", 2)
        b_pt = sem("b_pt")
        b_ptc = sem("b_ptc", 1)
        b_pv = sem("b_pv", RING)
        b_oc = sem("b_oc", 1)
        b_rc = sem("b_rc")
        b_nrm = sem("b_nrm", 2)
        b_ot = sem("b_ot", 1)
        b_att = sem("b_att", 2)
        b_out = sems("b_out", 2, 16)
        cs = []
        for layer in (0, 1):
            n = f"c{layer}_"
            cs.append(dict(
                x_in=sems(n + "x_in", 2), free=sem(n + "free", 2),
                y=sem(n + "y"), yT=sem(n + "yT"), yt=sem(n + "yt", 1), stat=sem(n + "stat"),
                tmp=sem(n + "tmp"), rstd=sem(n + "rstd"), norm=sem(n + "norm"), res=sem(n + "res", 1),
                xt=sem(n + "xt"), xT=sem(n + "xT"), lg=sem(n + "lg"), chain=sem(n + "chain"), ls=sem(n + "ls", 1), lc=sem(n + "lc"), pr=sem(n + "pr"), tmp2=sem(n + "tmp2"),
                ex=sem(n + "ex"), cw=sem(n + "cw"), ct=sem(n + "ct"), cT=sem(n + "cT"),
                h=sem(n + "h"), ge=sem(n + "ge", 2), cb=sem(n + "cb", 1), hc=sem(n + "hc"), used=sem(n + "used", 2),
                x2=sem(n + "x2", 1), out=sem(n + "out", 16), pout=sem(n + "pout", 32)))
            cs[-1].update(stat2=sem(n + "stat2"), rstd2=sem(n + "rstd2"), norm2=sem(n + "norm2"), sub2=sem(n + "sub2"),
                          parts=sem(n + "parts"), part=sem(n + "part", 1),
                          pt=sem(n + "pt"), pt2=sem(n + "pt2", 1), pT=sem(n + "pT", 2))

        def stats(dve, src, st, mv, chain, chained, then):
            for t in range(NT):
                dve.bn_stats(out=st[:, t, :], in_=src[:, t, :]).then_inc(chain, 1)
            for t in range(NT):
                dve.wait_ge(chain, chained + t + 1)
                alone(dve)
                last = dve.bn_aggr(out=mv[:, t, :], in_=st[:, t, :])
            last.then_inc(then, 1)

        def rstd(pool, mv, rs, eps, tmp, tmped, then):
            pool.tensor_scalar(out=rs[:, :], in0=mv[:, :, 1], scalar1=eps, scalar2=1.0,
                               op0=ALU.add, op1=ALU.mult).then_inc(tmp, 1)
            pool.wait_ge(tmp, tmped + 1)
            pool.tensor_tensor(out=rs[:, :], in0=rs[:, :], in1=k["mhalf"][0:TILE, 0:NT],
                               op=ALU.pow).then_inc(then, 1)

        def normalise(eng, src, mv, rs, dst, chain, count, then):
            wide = [TILE, NT, C]
            eng.tensor_tensor(out=dst[:, :, :], in0=src[:, :, :], in1=mv[:, :, 0:1].broadcast_to(wide),
                              op=ALU.subtract).then_inc(chain, 1)
            eng.wait_ge(chain, count)
            alone(eng)
            eng.tensor_tensor(out=dst[:, :, :], in0=dst[:, :, :], in1=rs[:, :].unsqueeze(2).broadcast_to(wide),
                              op=ALU.mult).then_inc(then, 1)

        def to_channels(pe, src, ps):
            for t in range(NT):
                last = pe.transpose(ps[0:C, t * TILE:(t + 1) * TILE], src[:, t, :], k["ident"][0:TILE, 0:TILE])
            return last


        def sp_a(sp, tau, i, step):
            s = tau * 2 + i
            if step == 0:
                sp.wait_ge(a_norm, s + 1)
                sp.dma_start(a_x[i][:], x_s[bass.ds(s, 1)].rearrange("a p t c -> (a p) t c")).then_inc(a_in[i], 16)
            if step == 5:
                b, y = split(sp, s, NWIN)
                put = a_out[i]
                sp.wait_ge(a_pool, s + 3)
                sp.dma_start(q_d[bass.ds(s * NWIN, NWIN)].rearrange("w c t -> c w t"), a_qk[i][0:C]).then_inc(put, 16)
                sp.dma_start(kv_d[bass.ds(s * NWIN, NWIN), :, 0:C].rearrange("w c t -> c w t"),
                             a_qk[i][C:128]).then_inc(put, 16)
                sp.dma_start(qr_d[bass.ds(s, 1)].rearrange("a c w -> (a c) w"), a_sum[i][0:C]).then_inc(put, 16)
                with nc.allow_non_contiguous_dma(reason="seven region sums a row"):
                    sp.dma_start(kr_d[bass.ds(b, 1), :, bass.ds(y * NWIN, NWIN)].rearrange("a c w -> (a c) w"),
                                 a_sum[i][C:128]).then_inc(put, 16)
                sp.wait_ge(a_ev, 4 * s + 12)
                sp.dma_start(kv_d[bass.ds(s * NWIN, NWIN), :, C:KV].rearrange("w t c -> t w c"),
                             a_v[i][:].rearrange("t w h c -> t w (h c)")).then_inc(put, 16)
                sp.dma_start(vpad_d[bass.ds(b, 1), :, bass.ds(y * RH + 1, RH), :].rearrange("a c h w -> (a c) h w"),
                             a_vT[i][:]).then_inc(put, 16)

        def dve_a(dve, tau, i, step):
            s = tau * 2 + i
            if step == 1:
                dve.wait_ge(a_in[i], 16 * (tau + 1))
                dve.wait_ge(a_norm, s + 1)
                alone(dve)
                stats(dve, a_x[i], a_st[i], a_mv[i], a_bn, 4 * s, a_stat)
            if step == 5:
                dve.wait_ge(a_ev, 4 * s + 10)
                dve.wait_ge(a_out[i], 96 * tau + 80)
                dve.tensor_reduce(out=a_sum[i][:, :], in_=a_qk[i][:], op=ALU.add, axis=AX.X).then_inc(a_pool, 1)

        def pool_a(pool, tau, i, step):
            s = tau * 2 + i
            if step == 1:
                pool.wait_ge(a_stat, s + 1)
                alone(pool)
                rstd(pool, a_mv[i], a_rs[i], 1e-6, a_tmp, s, a_rstd)
                pool.wait_ge(a_rstd, s + 1)
                pool.wait_ge(a_ev, 4 * s + 1)
                alone(pool)
                normalise(pool, a_x[i], a_mv[i], a_rs[i], a_xn[i], a_sub, s + 1, a_norm)

        def pe_a(pe, tau, i, step):
            s = tau * 2 + i
            if step == 3:
                pe.wait_ge(a_norm, s + 3)
                alone(pe)
                to_channels(pe, a_xn[i], a_ps).then_inc(a_full, 1)
                pe.wait_ge(a_ev, 4 * s + 9)
                alone(pe)
                pe.matmul(a_ps[:, 0:STRIP], k["wqkv"][:, 0:128], a_xT[i][:, :], start=True, stop=True).then_inc(a_full, 1)
                pe.wait_ge(a_ev, 4 * s + 10)
                alone(pe)
            if step == 4:
                for n in range(NWIN):
                    last = pe.matmul(a_ps[0:RTOK, n * C:(n + 1) * C], a_xT[i][:, n * RTOK:(n + 1) * RTOK],
                                     k["wqkv"][:, 128:192], start=True, stop=True)
                last.then_inc(a_full, 1)
                pe.wait_ge(a_ev, 4 * s + 11)
                alone(pe)
                pe.matmul(a_ps[0:C, 0:STRIP], k["wqkv"][:, 128:192],
                          a_xT[i][:, :].rearrange("c (w h q) -> c h w q", w=NWIN, h=RH),
                          start=True, stop=True).then_inc(a_full, 1)
                pe.wait_ge(a_ev, 4 * s + 12)
                alone(pe)

        def act_a(act, tau, i, step):
            s = tau * 2 + i
            if step == 3:
                act.wait_ge(a_full, 4 * s + 1)
                act.activation(a_xT[i][0:C, :].rearrange("c (w h q) -> c h w q", w=NWIN, h=RH),
                               a_ps[0:C, 0:STRIP].rearrange("c (h w q) -> c h w q", h=RH, w=NWIN), ACT.Copy).then_inc(a_ev, 1)
                act.wait_ge(a_out[i], 96 * tau + 80)
                act.wait_ge(a_full, 4 * s + 2)
                act.wait_ge(a_pool, s + 1)
                act.activation(a_qk[i][:].rearrange("c w t -> c (w t)"), a_ps[:, 0:STRIP], ACT.Copy).then_inc(a_ev, 1)
            if step == 4:
                act.wait_ge(a_full, 4 * s + 3)
                act.activation(a_v[i][:, :, :, 0:2 * HD], a_ps[0:RTOK, 0:STRIP].rearrange("t (w h c) -> t w h c", w=NWIN, h=HP), ACT.Copy).then_inc(a_ev, 1)
                act.wait_ge(a_full, 4 * s + 4)
                act.activation(a_vT[i][:, :, 1:W + 1], a_ps[0:C, 0:STRIP].rearrange("c (h w) -> c h w", h=RH),
                               ACT.Copy).then_inc(a_ev, 1)

        def sp_t(sp, tau, i, step, full):
            s = tau * 2 + i
            if step == 0:
                b, _ = split(sp, s, NWIN)
                for j in range(2):
                    strips = TURNS if full else tau + (4, 3 + i)[j]
                    sp.wait_ge(a_out[j], 96 * strips + 80)
                    alone(sp)
                sp.wait_ge(t_ev, s + 1)
                sp.dma_start(t_q[i][:], qr_d[bass.ds(s, 1)].rearrange("a c w -> (a c) w")).then_inc(t_in[i], 16)
                sp.dma_start(t_k[i][:], kr_d[bass.ds(b, 1)].rearrange("a c w -> (a c) w")).then_inc(t_in[i], 16)
            if step == 3:
                sp.wait_ge(t_idx, s + 3)
                sp.dma_start(idx_d[bass.ds(s * NWIN, NWIN)], t_i[i][:]).then_inc(t_out[i], 16)

        def pe_t(pe, tau, i, step):
            s = tau * 2 + i
            if step == 1:
                pe.wait_ge(t_in[i], 32 * (tau + 1))
                alone(pe)
                pe.matmul(a_ps[0:NWIN, 0:REG], t_q[i][:, :], t_k[i][:, :], start=True, stop=True).then_inc(t_full, 1)
                pe.wait_ge(t_ev, s + 3)
                alone(pe)

        def act_t(act, tau, i, step):
            s = tau * 2 + i
            if step == 1:
                act.wait_ge(t_full, s + 1)
                act.wait_ge(t_idx, s + 1)
                act.activation(t_a[i][:, :], a_ps[0:NWIN, 0:REG], ACT.Copy).then_inc(t_ev, 1)

        def dve_t(dve, tau, i, step):
            s = tau * 2 + i
            if step == 2:
                dve.wait_ge(t_ev, s + 3)
                alone(dve)
                dve.max(out=t_v[i][:, :], in_=t_a[i][:, :]).then_inc(t_max, 1)
                dve.wait_ge(t_out[i], 16 * tau + 16)
                dve.wait_ge(t_max, s + 1)
                alone(dve)
                dve.max_index(out=t_i[i][:, :], in_max=t_v[i][:, :], in_values=t_a[i][:, :]).then_inc(t_idx, 1)

        def sp_gather(sp, tau, r):
            reg, slot = tau * SLOTS + r, r % RING
            b, _ = split(sp, reg, REG)
            got = b_in[slot]
            if r % NWIN == 0:
                sp.wait_ge(t_out[(r // NWIN) % 2], 16 * (tau + r // SLOTS) + 32)
                alone(sp)
            sp.wait_ge(b_pv, reg + 1)
            alone(sp)
            best = [sp.value_load(idx_d[bass.ds(reg, 1), j:j + 1], min_val=0, max_val=REG - 1) for j in range(TOPK)]
            for j in range(TOPK):
                src = sp.snap(best[j] + b * REG)
                half = (j % 2) * RTOK
                sp.dma_start(b_kv[slot][half:half + RTOK, j // 2, :],
                             kv_d[bass.ds(src, 1)].rearrange("a p c -> (a p) c")).then_inc(got, 16)
            for half in (0, C):
                sp.dma_start(b_q[slot][half:half + C, :], q_d[bass.ds(reg, 1)].rearrange("a c t -> (a c) t")).then_inc(got, 16)

        def pool_spread(pool, tau, r):
            reg = tau * SLOTS + r
            pool.wait_ge(b_in[r % RING], 96 * (tau * 2 + r // RING + 1))
            pool.wait_ge(b_qk, reg + 1)
            pool.tensor_tensor(out=b_qe[r % 2][:, :, :],
                               in0=b_q[r % RING][:, :].unsqueeze(1).broadcast_to([128, 2 * NHEAD, RTOK]),
                               in1=k["head"][:, :].unsqueeze(2).broadcast_to([128, 2 * NHEAD, RTOK]),
                               op=ALU.mult).then_inc(b_qx, 1)

        def pe_scores(pe, tau, r):
            reg = tau * SLOTS + r
            pe.wait_ge(b_in[r % RING], 96 * (tau * 2 + r // RING + 1))
            pe.wait_ge(b_qx, reg + 1)
            pe.wait_ge(b_sc, reg + 1)
            alone(pe)
            for half in range(2):
                for t in range(HP):
                    head = half * NHEAD + 2 * t
                    last = pe.matmul(s_ps[half][:, t * 128:(t + 1) * 128],
                                     b_qe[r % 2][:, head:head + 2, :].rearrange("c h t -> c (h t)"),
                                     b_kv[r % RING][:, :, 0:RTOK], start=True, stop=True)
            last.then_inc(b_qk, 1)

        def act_scores(act, tau, r):
            reg = tau * SLOTS + r
            act.wait_ge(b_exp, reg + 1)
            act.wait_ge(b_qk, reg + 3)
            for half in range(2):
                last = act.activation(b_s[r % 2][:].rearrange("p t (a h q) -> p h t a q", h=2, q=RTOK)[:, half],
                                      s_ps[half][:, :].rearrange("p (t a q) -> p t a q", t=HP, a=2), ACT.Copy)
            last.then_inc(b_sc, 1)

        def dve_select(dve, tau, r, ready):
            reg, p = tau * SLOTS + r, r % 2
            chain = b_chain
            dve.wait_ge(b_sc, reg + 2)
            dve.wait_ge(b_prob, reg + 1)
            alone(dve)
            rounds = KSEL // 8
            for rnd in range(rounds):
                src = b_s[p] if rnd == 0 else b_r[p]
                for t in range(HP):
                    if rnd:
                        dve.wait_ge(chain, (2 * rnd - 1) * HP + t + 1)
                        alone(dve)
                    dve.max(out=b_v8[p][:, t, 8 * rnd:8 * rnd + 8], in_=src[:, t, :]).then_inc(chain, 1)
                if rnd == rounds - 1 and ready is not None:
                    dve_recip(dve, tau, ready)
                for t in range(HP):
                    dve.wait_ge(chain, 2 * rnd * HP + t + 1)
                    last = dve.match_replace(out=b_r[p][:, t, :], in_to_replace=b_v8[p][:, t, 8 * rnd:8 * rnd + 8],
                                             in_values=src[:, t, :], imm_value=GONE)
                    if rnd < rounds - 1:
                        last.then_inc(chain, 1)
            last.then_inc(b_sel, 1)
            dve.sem_clear(chain)

        def dve_recip(dve, tau, r):
            reg = tau * SLOTS + r
            dve.wait_ge(b_oc, reg + 2)
            alone(dve)
            dve.wait_ge(b_nrm, reg + 2)
            alone(dve)
            dve.reciprocal(b_rec[:, :], b_o[r % 2][:, :, 2 * HD]).then_inc(b_rc, 1)

        def dve_norm(dve, tau, r):
            reg = tau * SLOTS + r
            dve.wait_ge(b_ot, reg + 1)
            alone(dve)
            dve.wait_ge(b_rc, reg + 1)
            alone(dve)
            for half in range(2):
                part = slice(half * RTOK, half * RTOK + RTOK)
                own = b_o[r % 2][part, :, half * HD:(half + 1) * HD]
                last = dve.tensor_tensor(out=b_on[part, :, :], in0=own,
                                         in1=b_rec[part, :].unsqueeze(2).broadcast_to([RTOK, HP, HD]), op=ALU.mult)
            last.then_inc(b_nrm, 1)

        def act_exp(act, tau, r):
            reg, p = tau * SLOTS + r, r % 2
            act.wait_ge(b_sel, reg + 1)
            act.activation(b_nm[p][:, :], b_v8[p][:, :, 0], ACT.Copy, scale=-1.0).then_inc(b_neg, 1)
            act.wait_ge(b_prob, reg + 1)
            act.wait_ge(b_neg, reg + 1)
            for t in range(HP):
                last = act.activation(b_e[p][:, t, :], b_s[p][:, t, :], ACT.Exp, bias=b_nm[p][:, t:t + 1])
            last.then_inc(b_exp, 1)

        def pool_mask(pool, tau, r):
            reg, p = tau * SLOTS + r, r % 2
            pool.wait_ge(b_sel, reg + 1)
            alone(pool)
            pool.tensor_scalar(out=b_r[p][:, :, :], in0=b_r[p][:, :, :], scalar1=GONE, scalar2=None,
                               op0=ALU.is_le).then_inc(b_msk, 1)

        def pool_prob(pool, tau, r):
            reg, p = tau * SLOTS + r, r % 2
            pool.wait_ge(b_msk, reg + 1)
            pool.wait_ge(b_exp, reg + 3)
            pool.tensor_tensor(out=b_e[p][:, :, :], in0=b_e[p][:, :, :], in1=b_r[p][:, :, :],
                               op=ALU.mult).then_inc(b_prob, 1)

        def pe_turn(pe, tau, r, half):
            reg, p = tau * SLOTS + r, r % 2
            if half == 0:
                pe.wait_ge(b_prob, reg + 3)
                alone(pe)
            pe.wait_ge(b_ptc, 2 * reg + half + 1)
            alone(pe)
            for t in range(2 * half, 2 * half + 2):
                for c in range(2):
                    col = (t % 2) * 256 + c * 128
                    last = pe.transpose(pT_ps[:, col:col + 128], b_e[p][:, t, c * 128:(c + 1) * 128], k["ident"][:, :])
            last.then_inc(b_pt, 1)

        def act_turn(act, tau, r, half):
            reg = tau * SLOTS + r
            if half == 0:
                act.wait_ge(b_pv, reg + 7)
            act.wait_ge(b_pt, 2 * reg + half + 1)
            act.activation(b_pT[half][:, :], pT_ps[:, :], ACT.Copy).then_inc(b_ptc, 1)

        def pe_values(pe, tau, r):
            reg = tau * SLOTS + r
            pe.wait_ge(b_att, reg + 1)
            alone(pe)
            pe.wait_ge(b_oc, reg + 1)
            alone(pe)
            for t in range(HP):
                if t % 2 == 0:
                    pe.wait_ge(b_ptc, 2 * reg + t // 2 + 2)
                    alone(pe)
                for c in range(2):
                    last = pe.matmul(o_ps[:, t * VH:(t + 1) * VH],
                                     b_pT[t // 2][:, (t % 2) * 256 + c * 128:(t % 2) * 256 + (c + 1) * 128],
                                     b_kv[r % RING][:, c, C + t * VH:C + (t + 1) * VH], start=(c == 0), stop=(c == 1))
            last.then_inc(b_pv, 1)

        def act_values(act, tau, r):
            reg = tau * SLOTS + r
            act.wait_ge(b_nrm, reg + 1)
            act.wait_ge(b_pv, reg + 8)
            act.activation(b_o[r % 2][:].rearrange("p t c -> p (t c)"), o_ps[:, 0:HP * VH], ACT.Copy).then_inc(b_oc, 1)

        def pe_out(pe, tau, r, newest):
            reg = tau * SLOTS + r
            pe.wait_ge(b_oc, tau * SLOTS + newest + 2)
            alone(pe)
            pe.wait_ge(b_att, reg + 2)
            alone(pe)
            pe.wait_ge(b_nrm, reg + 3)
            alone(pe)
            pe.transpose(o_ps[0:32, 0:128], b_on[:, :, :].rearrange("p t c -> p (t c)"), k["ident"][:, :]).then_inc(b_ot, 1)

        def act_out(act, tau, r):
            reg, i, win = tau * SLOTS + r, (r // NWIN) % 2, r % NWIN
            if win == 0:
                act.wait_ge(b_out[i], 16 * tau + 16)
            act.wait_ge(b_ot, reg + 2)
            act.activation(b_at[i][:, :, :, win * RH:(win + 1) * RH],
                           o_ps[0:32, 0:128].rearrange("c (j h q) -> c j h q", j=2, h=RH), ACT.Copy).then_inc(b_att, 1)

        def sp_strip(sp, tau, i):
            s = tau * 2 + i
            sp.wait_ge(b_att, NWIN * (s + 1) + 2)
            sp.dma_start(at_d[bass.ds(s, 1)].rearrange("a j c f -> (a c) j f"),
                         b_at[i][:].rearrange("c j h w -> c j (h w)")).then_inc(b_out[i], 16)

        UP, DOWN, TURN, TURNED, GATE, GATED, LOW, LOWED = 10, 20, 30, 31, 32, 33, 34, 35
        groups = (NE // 2, NE)
        w1, w2, b1 = (k["w1_0"], k["w1_1"]), (k["w2_0"], k["w2_1"]), (k["b1_0"], k["b1_1"])
        gate = (k["gate_0"], k["gate_1"])

        LOADS = (16 * 7, 16 * 4)

        def sp_c(sp, tau, i, step, layer, last):
            S, D = cs[layer], cb_[layer]
            s = tau * 2 + i
            if step == 0:
                b, y = split(sp, s, NWIN)
                got = S["x_in"][i]
                sp.wait_ge(S["free"], s + 1)
                alone(sp)
                if layer == 0:
                    sp.dma_start(D["x"][i][:], x_s[bass.ds(s, 1)].rearrange("a p t c -> (a p) t c")).then_inc(got, 16)
                    pad = vpad_d[bass.ds(b, 1)].rearrange("a c h w -> (a c) h w")
                    sp.dma_start(c_win[i][0:C], pad[:, bass.ds(y * RH, RH + 2), :]).then_inc(got, 16)
                    sp.dma_start(c_win[i][C:128, 0:RH], pad[:, bass.ds(y * RH + 1, RH), :]).then_inc(got, 16)
                    sp.dma_start(c_row[i][0:C], pad[:, bass.ds(y * RH + 2, RH), :]).then_inc(got, 16)
                    sp.dma_start(c_row[i][C:128, :, 0:PW - 1], pad[:, bass.ds(y * RH + 2, RH), 1:PW]).then_inc(got, 16)
                    sp.dma_start(c_cor[i][0:C], pad[:, bass.ds(y * RH + 2, RH), 2:PW]).then_inc(got, 16)
                    sp.wait_ge(b_out[i], 16 * tau + 32)
                    sp.dma_start(c_cor[i][C:128].rearrange("c h w -> c (h w)"),
                                 at_d[bass.ds(s, 1)].rearrange("a j c f -> (a j c) f")).then_inc(got, 16)
                else:
                    sp.wait_ge(cs[0]["out"], 16 * s + 32)
                    sp.dma_start(D["x"][i][:], x2_d[bass.ds(s, 1)].rearrange("a p (t c) -> (a p) t c", t=NT)).then_inc(got, 16)
                    sp.wait_ge(cs[0]["pout"], 32 * (2 * TURNS if last else s + 2) + 32)
                    pad = cpad_d[bass.ds(b, 1)].rearrange("a c h w -> (a c) h w")
                    sp.dma_start(c_hm[i][:], pad[0:2 * C, bass.ds(y * RH, RH + 2), :]).then_inc(got, 16)
                    sp.dma_start(c_lo[i][0:C], pad[2 * C:3 * C, bass.ds(y * RH, RH + 2), :]).then_inc(got, 16)
                    sp.dma_start(c_lo[i][C:128, 0:RH], pad[2 * C:3 * C, bass.ds(y * RH + 1, RH), :]).then_inc(got, 16)
            if step == 9:
                b, y = split(sp, s, NWIN)
                sp.wait_ge(S["x2"], s + 2)
                alone(sp)
                if layer == 0:
                    sp.dma_start(x2_d[bass.ds(s, 1)].rearrange("a p (t c) -> (a p) t c", t=NT), D["x2"][:]).then_inc(S["out"], 16)
                    sp.wait_ge(S["pT"], 2 * s + 4)
                    pad = cpad_d[bass.ds(b, 1), :, bass.ds(y * RH + 1, RH), :].rearrange("a c h w -> (a c) h w")
                    sp.dma_start(pad[0:2 * C], c_hmp[:]).then_inc(S["pout"], 16)
                    sp.dma_start(pad[2 * C:3 * C], c_lop[:]).then_inc(S["pout"], 16)
                else:
                    sp.dma_start(out_s[bass.ds(s, 1)].rearrange("a p t c -> (a p) t c"), D["x2"][:]).then_inc(S["out"], 16)

        def pe_c(pe, tau, i, step, layer, other):
            S, O, D, G = cs[layer], cs[1 - layer], cb_[layer], groups[layer]
            s = tau * 2 + i
            if step == 0:
                pe.wait_ge(S["x_in"][i], LOADS[layer] * (tau + 1))
                alone(pe)
                if layer == 0:
                    moving = [c_win[i][:, 0:RH, dx:dx + W] for dx in range(3)] + [c_row[i][:, :, 0:W], c_cor[i][:]]
                    for j in range(5):
                        last = pe.matmul(h_ps[0:C, 0:STRIP], lepe_tap[:, j, :], moving[j], start=(j == 0), stop=(j == 4))
                else:
                    for j in range(9):
                        pe.matmul(h_ps[0:C, 0:STRIP], conv_tap[:, j, :], c_hm[i][:, j // 3:j // 3 + RH, j % 3:j % 3 + W],
                                  start=(j == 0), stop=False)
                    for dx in range(3):
                        pe.matmul(h_ps[0:C, 0:STRIP], conv_low[:, dx, :], c_lo[i][:, 0:RH, dx:dx + W], start=False, stop=False)
                        last = pe.matmul(h_ps[0:C, 0:STRIP], conv_low[0:C, 3 + dx, :], c_lo[i][0:C, 2:2 + RH, dx:dx + W],
                                         start=False, stop=(dx == 2))
                last.then_inc(S["y"], 1)
            if step == TURN:
                pe.wait_ge(S["yT"], s + 1)
                alone(pe)
                for t in range(NT):
                    last = pe.transpose(a_ps[0:TILE, t * C:(t + 1) * C], D["yT"][:, t * TILE:(t + 1) * TILE], k["ident"][0:C, 0:C])
                last.then_inc(S["yt"], 1)
            if step == TURNED:
                pe.wait_ge(S["pr"], s + 1)
                alone(pe)
            if step == 2:
                pe.wait_ge(S["norm"], s + 1)
                alone(pe)
                to_channels(pe, D["xn"], g_ps).then_inc(S["xt"], 1)
            if step == GATE:
                pe.wait_ge(S["xT"], s + 1)
                alone(pe)
                for t in range(NT):
                    last = pe.matmul(a_ps[0:TILE, t * NE:(t + 1) * NE], D["xT"][:, t * TILE:(t + 1) * TILE], gate[layer][:, :],
                                     start=True, stop=True)
                last.then_inc(S["lg"], 1)
            if step == GATED:
                pe.wait_ge(S["lc"], s + 1)
                alone(pe)
            if step == 4:
                pe.wait_ge(S["cw"], s + 1)
                alone(pe)
                for t in range(NT):
                    last = pe.matmul(h_ps[0:3 * NE, t * TILE:(t + 1) * TILE], D["cw3"][:, t, :, :].rearrange("p a e -> p (a e)"),
                                     ident_b[0:TILE, 0:TILE], start=True, stop=True)
                last.then_inc(S["ct"], 1)

            if UP <= step < UP + G:
                g = step - UP
                n = s * G + g
                bank = (h_ps, a_ps)[g % 2]
                if g == 0:
                    pe.wait_ge(S["cT"], s + 1)
                    alone(pe)
                pe.wait_ge(S["ge"], n + 1)
                alone(pe)
                pe.matmul(bank[:, 0:STRIP], w1[layer][:, g, :], D["xT"][:, :], start=True, stop=True).then_inc(S["h"], 1)
                pe.wait_ge(S["cb"], n + 1)
                alone(pe)
                pe.matmul(g_ps[:, 0:STRIP], sel_b[layer][:, g, :], D["cwT"][:, :], start=True, stop=True).then_inc(S["h"], 1)
            if DOWN <= step < DOWN + G:
                g = step - DOWN
                if g == 0:
                    pe.wait_ge(S["x2"], s + 1)
                    alone(pe)
                    if other is not None:
                        pe.wait_ge(O["x2"], other + 2)
                        alone(pe)
                    for t in range(NT):
                        for part in range(3):
                            pe.matmul(y_ps[0:TILE, t * C:(t + 1) * C], D["cwT"][:, t * TILE:(t + 1) * TILE], b2_b[layer][:, part, :],
                                      start=(t == 0 and part == 0), stop=False, skip_group_check=True)
                pe.wait_ge(S["hc"], s * G + g + 1)
                alone(pe)
                for t in range(NT):
                    last = pe.matmul(y_ps[0:TILE, t * C:(t + 1) * C], D["h"][g % 2][:, t * TILE:(t + 1) * TILE],
                                     w2[layer][:, g, :], start=False, stop=(g == G - 1), skip_group_check=True)
                last.then_inc(S["used"], 1)
            if step == 8 and layer == 0:
                pe.wait_ge(S["part"], s + 2)
                alone(pe)
                for t in range(NT):
                    last = pe.matmul(g_ps[:, t * TILE:(t + 1) * TILE], c_x3[:, t, 0:2, :].rearrange("p a c -> p (a c)"),
                                     ident_b[0:TILE, 0:TILE], start=True, stop=True)
                last.then_inc(S["pt"], 1)
            if step == LOW:
                pe.wait_ge(S["pT"], 2 * s + 3)
                alone(pe)
                for t in range(NT):
                    last = pe.matmul(g_ps[0:C, t * TILE:(t + 1) * TILE], c_x3[:, t, 2, :], ident_b[0:TILE, 0:TILE], start=True, stop=True)
                last.then_inc(S["pt2"], 1)
            if step == LOWED:
                pe.wait_ge(S["pT"], 2 * s + 4)
                alone(pe)

        def act_c(act, tau, i, step, layer):
            S, D, G = cs[layer], cb_[layer], groups[layer]
            s = tau * 2 + i
            if step == 0:
                act.wait_ge(S["y"], s + 1)
                act.wait_ge(S["yt"], s + 1)
                if layer == 0:
                    act.activation(D["yT"][:, :], h_ps[0:C, 0:STRIP], ACT.Identity, bias=out_bias[:, 0:1]).then_inc(S["yT"], 1)
                else:
                    act.activation(D["yT"][:, :], h_ps[0:C, 0:STRIP], ACT.Copy).then_inc(S["yT"], 1)
            if step == TURN:
                act.wait_ge(S["yt"], s + 2)
                act.wait_ge(S["free"], s + 2)
                act.activation(D["pr"][:, :, :].rearrange("p t c -> p (t c)"), a_ps[0:TILE, 0:NT * C], ACT.Copy).then_inc(S["pr"], 1)
            if step == 2:
                act.wait_ge(S["xt"], s + 1)
                act.activation(D["xT"][0:C, :], g_ps[0:C, 0:STRIP], ACT.Copy).then_inc(S["xT"], 1)
            if step == GATE:
                act.wait_ge(S["lg"], s + 1)
                act.wait_ge(S["ls"], s + 1)
                act.activation(D["lg"][:, :, :].rearrange("p t e -> p (t e)"), a_ps[0:TILE, 0:NT * NE], ACT.Copy).then_inc(S["lc"], 1)
            if step == 3:
                act.wait_ge(S["ls"], s + 2)
                act.activation(D["p"][:, :, :], D["l"][:, :, :], ACT.Exp).then_inc(S["ex"], 1)
            if step == 4:
                act.wait_ge(S["ct"], s + 1)
                act.activation(D["cwT"][0:3 * NE, :], h_ps[0:3 * NE, 0:STRIP], ACT.Copy).then_inc(S["cT"], 1)
            if UP <= step < UP + G:
                g = step - UP
                n = s * G + g
                act.wait_ge(S["used"], n + 1)
                act.wait_ge(S["h"], 2 * n + 1)
                act.activation(D["h"][g % 2][:, :], (h_ps, a_ps)[g % 2][:, 0:STRIP], ACT.Gelu, bias=b1[layer][:, g:g + 1]).then_inc(S["ge"], 1)
                act.wait_ge(S["h"], 2 * n + 2)
                act.activation(D["cb"][g % 2][:, :], g_ps[:, 0:STRIP], ACT.Copy).then_inc(S["cb"], 1)
            if step == 8 and layer == 0:
                act.wait_ge(S["pt"], s + 1)
                act.wait_ge(S["pout"], 32 * s + 32)
                act.activation(c_hmp[:, :, 1:W + 1], g_ps[:, 0:STRIP].rearrange("c (h w) -> c h w", h=RH), ACT.Copy).then_inc(S["pT"], 1)
            if step == LOW:
                act.wait_ge(S["pt2"], s + 2)
                act.activation(c_lop[:, :, 1:W + 1], g_ps[0:C, 0:STRIP].rearrange("c (h w) -> c h w", h=RH),
                               ACT.Copy).then_inc(S["pT"], 1)

        def pool_c(pool, tau, i, step, layer):
            S, D, G = cs[layer], cb_[layer], groups[layer]
            s = tau * 2 + i
            if step == 1:
                pool.wait_ge(S["stat"], s + 1)
                alone(pool)
                rstd(pool, D["mv"], D["rs"], 1e-5, S["tmp"], s, S["rstd"])
            if step == 2 and layer == 0:
                pool.wait_ge(S["norm"], s + 1)
                pool.tensor_tensor(out=D["xr"][i][:, :, :], in0=D["tok"][i][:, :, :], in1=D["xn"][:, :, :], op=ALU.add).then_inc(S["res"], 1)
            if UP <= step < UP + G:
                g = step - UP
                pool.wait_ge(S["cb"], s * G + g + 2)
                pool.tensor_tensor(out=D["h"][g % 2][:, :], in0=D["h"][g % 2][:, :], in1=D["cb"][g % 2][:, :],
                                   op=ALU.mult).then_inc(S["hc"], 1)
            if step == 7 and layer == 0:
                pool.wait_ge(S["stat2"], s + 1)
                alone(pool)
                rstd(pool, D["mv2"], D["rs2"], 1e-6, S["tmp2"], s, S["rstd2"])
            if step == 8 and layer == 0:
                pool.wait_ge(S["rstd2"], s + 1)
                alone(pool)
                normalise(pool, D["x2"], D["mv2"], D["rs2"], D["xm"], S["sub2"], s + 1, S["norm2"])
                pool.wait_ge(S["norm2"], s + 1)
                pool.wait_ge(S["pt2"], s + 1)
                alone(pool)
                pool.tensor_copy(c_x3[:, :, 0, :], D["xm"][:, :, :]).then_inc(S["parts"], 1)
                pool.wait_ge(S["parts"], 3 * s + 1)
                pool.tensor_tensor(out=c_xd[:, :, :], in0=D["xm"][:, :, :], in1=c_x3[:, :, 0, :], op=ALU.subtract).then_inc(S["parts"], 1)
                pool.wait_ge(S["parts"], 3 * s + 2)
                alone(pool)
                pool.tensor_copy(c_x3[:, :, 1, :], c_xd[:, :, :]).then_inc(S["parts"], 1)
                pool.wait_ge(S["parts"], 3 * s + 3)
                pool.tensor_tensor(out=c_x3[:, :, 2, :], in0=c_xd[:, :, :], in1=c_x3[:, :, 1, :], op=ALU.subtract).then_inc(S["part"], 1)

        def dve_c(dve, tau, i, step, layer):
            S, D, G = cs[layer], cb_[layer], groups[layer]
            s = tau * 2 + i
            tok, xn, x2, mv, st, p, cw, m = D["tok"][i], D["xn"], D["x2"], D["mv"], D["st"], D["p"], D["cw"], D["m"]
            by_expert = [TILE, NT, NE]
            count = [0]

            def link(ins):
                count[0] += 1
                ins.then_inc(S["chain"], 1)
                dve.wait_ge(S["chain"], count[0])

            def mean_var(src, mv, then):
                for t in range(NT):
                    ins = dve.bn_stats(out=st[:, t, :], in_=src[:, t, :])
                    if t < NT - 1:
                        ins.then_inc(S["chain"], 1)
                        count[0] += 1
                link(ins)
                for t in range(NT):
                    ins = dve.bn_aggr(out=mv[:, t, :], in_=st[:, t, :])
                ins.then_inc(then, 1)

            dve.sem_clear(S["chain"])
            if step == 1:
                dve.wait_ge(S["x_in"][i], LOADS[layer] * (tau + 1))
                dve.wait_ge(S["pr"], s + 1)
                alone(dve)
                if layer == 0:
                    dve.wait_ge(S["res"], s + 1)
                    alone(dve)
                link(dve.tensor_tensor(out=tok[:, :, :], in0=D["x"][i][:, :, :],
                                       in1=D["pr"][:, :, :], op=ALU.add))
                dve.sem_inc(S["free"], 1)
                mean_var(tok, mv, S["stat"])
            if step == 2:
                dve.wait_ge(S["rstd"], s + 1)
                alone(dve)
                normalise(dve, tok, mv, D["rs"], xn, S["chain"], 1, S["norm"])
            if step == 3:
                dve.wait_ge(S["lc"], s + 1)
                alone(dve)
                lg = D["lg"][:, :, :]
                link(dve.tensor_reduce(out=D["lm"][:, :], in_=lg, op=ALU.max, axis=AX.X))
                dve.tensor_tensor(out=D["l"][:, :, :], in0=lg, in1=D["lm"][:, :].unsqueeze(2).broadcast_to(by_expert),
                                  op=ALU.subtract).then_inc(S["ls"], 1)
            if step == 4:
                dve.wait_ge(S["ex"], s + 1)
                alone(dve)
                link(dve.tensor_reduce(out=D["z"][:, :], in_=p[:, :, :], op=ALU.add, axis=AX.X))
                link(dve.reciprocal(D["rz"][:, :], D["z"][:, :]))
                link(dve.tensor_tensor(out=p[:, :, :], in0=p[:, :, :], in1=D["rz"][:, :].unsqueeze(2).broadcast_to(by_expert), op=ALU.mult))
                for t in range(NT):
                    ins = dve.max(out=D["pv"][:, t, :], in_=p[:, t, :])
                link(ins)
                for t in range(NT):
                    ins = dve.max_index(out=D["pi"][:, t, :], in_max=D["pv"][:, t, :], in_values=p[:, t, :])
                link(ins)
                link(dve.tensor_copy(D["pf"][:, :, :], D["pi"][:, :, :]))
                for j in range(2):
                    ins = dve.tensor_tensor(out=m[j][:, :, :], in0=k["iota"][0:TILE, :].unsqueeze(1).broadcast_to(by_expert),
                                            in1=D["pf"][:, :, j:j + 1].broadcast_to(by_expert), op=ALU.is_equal)
                link(ins)
                link(dve.tensor_tensor(out=m[0][:, :, :], in0=m[0][:, :, :], in1=m[1][:, :, :], op=ALU.add))
                ins = dve.tensor_tensor(out=cw[:, :, :], in0=m[0][:, :, :], in1=p[:, :, :], op=ALU.mult)
                if layer == 0:
                    link(ins)
                    link(dve.tensor_tensor(out=D["z"][:, :], in0=D["pv"][:, :, 0], in1=D["pv"][:, :, 1], op=ALU.add))
                    link(dve.tensor_scalar(out=D["z"][:, :], in0=D["z"][:, :], scalar1=1e-12, scalar2=None, op0=ALU.max))
                    link(dve.reciprocal(D["rz"][:, :], D["z"][:, :]))
                    ins = dve.tensor_tensor(out=cw[:, :, :], in0=cw[:, :, :], in1=D["rz"][:, :].unsqueeze(2).broadcast_to(by_expert), op=ALU.mult)
                link(ins)
                cw3, cwd = D["cw3"], D["cwd"]
                link(dve.tensor_copy(cw3[:, :, 0, :], cw[:, :, :]))
                link(dve.tensor_tensor(out=cwd[:, :, :], in0=cw[:, :, :], in1=cw3[:, :, 0, :], op=ALU.subtract))
                link(dve.tensor_copy(cw3[:, :, 1, :], cwd[:, :, :]))
                dve.tensor_tensor(out=cw3[:, :, 2, :], in0=cwd[:, :, :], in1=cw3[:, :, 1, :], op=ALU.subtract).then_inc(S["cw"], 1)
            if step == 7:
                dve.wait_ge(S["out"], 16 * s + 16)
                if layer == 0:
                    dve.wait_ge(S["part"], s + 1)
                    alone(dve)
                dve.wait_ge(S["used"], (s + 1) * G + 2)
                alone(dve)
                moe = y_ps[0:TILE, 0:NT * C].rearrange("p (t c) -> p t c", t=NT)
                if layer == 0:
                    dve.wait_ge(S["res"], s + 2)
                    alone(dve)
                    link(dve.tensor_tensor(out=x2[:, :, :], in0=D["xr"][i][:, :, :], in1=moe, op=ALU.add))
                    dve.sem_inc(S["x2"], 1)
                    mean_var(x2, D["mv2"], S["stat2"])
                else:
                    dve.tensor_tensor(out=x2[:, :, :], in0=tok[:, :, :], in1=moe, op=ALU.add).then_inc(S["x2"], 1)

        B_START = 5 * SLOTS
        PLACES = dict(
            sp={("a", 0): 0.9, ("a", 5): 11.9, ("t", 0): 54.8, ("t", 3): 62.8, ("c0", 0): 80.7, ("c0", 9): 98.7,
                ("c1", 0): 106.66, ("c1", 9): 120.66},
            dve={("a", 1): 4.9, ("a", 5): 10.9, ("t", 2): 61.8,
                 ("c0", 1): 85.7, ("c0", 2): 86.7, ("c0", 3): 88.7, ("c0", 4): 90.7, ("c0", 7): 94.7,
                 ("c1", 1): 109.66, ("c1", 2): 111.66, ("c1", 3): 113.66, ("c1", 4): 114.66, ("c1", 7): 119.66},
            pool={("a", 1): 4.9, ("c0", 1): 85.7, ("c0", 2): 86.7, ("c0", 7): 94.7, ("c0", 8): 96.7, ("c1", 1): 109.66},
            pe={("a", 3): 7.9, ("a", 4): 8.9, ("t", 1): 59.8,
                ("c0", 0): 83.1, ("c0", TURN): 83.5, ("c0", TURNED): 83.68, ("c0", 2): 86.66, ("c0", GATE): 87.05,
                ("c0", GATED): 87.31, ("c0", 4): 90.64, ("c0", 8): 97.3, ("c0", LOW): 97.55, ("c0", LOWED): 97.69,
                ("c1", 0): 107.1, ("c1", TURN): 107.5, ("c1", TURNED): 107.68, ("c1", 2): 111.695, ("c1", GATE): 112.05,
                ("c1", GATED): 112.31, ("c1", 4): 114.64},
            act={("a", 3): 7.9, ("a", 4): 8.9, ("t", 1): 59.8,
                 ("c0", 0): 83.3, ("c0", TURN): 83.52, ("c0", 2): 86.68, ("c0", GATE): 87.12, ("c0", 3): 88.7,
                 ("c0", 4): 90.66, ("c0", 8): 97.35, ("c0", LOW): 97.57,
                 ("c1", 0): 107.3, ("c1", TURN): 107.52, ("c1", 2): 111.7, ("c1", GATE): 112.12, ("c1", 3): 113.68,
                 ("c1", 4): 114.66})
        for layer, slot, gs in ((0, 91, (0, 1)), (0, 92, (2, 3)), (1, 115, (0, 1, 2)), (1, 116, (3, 4, 5)), (1, 117, (6, 7))):
            for g, up, down, act_up, pool_up in zip(gs, (0.1, 0.32, 0.5), (0.45, 0.62, 0.64), (0.15, 0.35, 0.5), (0.25, 0.45, 0.55)):
                PLACES["pe"][f"c{layer}", UP + g] = slot + up
                PLACES["pe"][f"c{layer}", DOWN + g] = slot + down
                PLACES["act"][f"c{layer}", UP + g] = slot + act_up
                PLACES["pool"][f"c{layer}", UP + g] = slot + pool_up
        Y_LAG = (4, 3)

        def crossings(place):
            return [(r, (r - int(place)) // NWIN) for r in range(SLOTS) if (r - int(place)) % NWIN == 0]

        def turns_of(c):
            return -(c // 2), -((c - NSTRIP) // 2)

        B_TURNS = (B_START // SLOTS, B_START // SLOTS + TURNS)
        MARKS = sorted({B_TURNS[0], B_TURNS[0] + 1, B_TURNS[1] - 1, B_TURNS[1]} |
                       {m for table in PLACES.values() for p in table.values() for _, c in crossings(p) for m in turns_of(c)})

        def steps_at(n, table, slot, lo, hi):
            found = [(p % 1, st, step, c) for (st, step), p in table.items() if lo < p % 1 < hi
                     for r, c in crossings(p) if r == slot and turns_of(c)[0] <= n < turns_of(c)[1]]
            return [f[1:] for f in sorted(found)]

        def run(eng, body):
            for lo, hi in zip(MARKS, MARKS[1:]):
                if hi - lo == 1:
                    body(lo, lo)
                else:
                    with eng.Fori(lo, hi) as n:
                        body(n, lo)

        def steps(eng, name, n, lo, slot, fs, after, before):
            for stage, step, c in steps_at(lo, PLACES[name], slot, after, before):
                tau, i = n + c // 2, c % 2
                args = ()
                if name == "sp" and stage == "t":
                    args = (2 * lo + c + NWIN - 1 >= NSTRIP,)
                if stage in ("c0", "c1"):
                    args = (int(stage[1]),)
                    if name == "sp":
                        args += (2 * lo + c + 2 > NSTRIP,)
                    if name == "pe":
                        o = c + (-Y_LAG[0], Y_LAG[1])[args[0]]
                        o_there = 0 <= 2 * lo + o < NSTRIP
                        args += ((n * 2 + o) if o_there else None,)
                fs[stage[0]](eng, tau, i, step, *args)

        names = list(w)
        with nc.Block() as block:
            @block.sync
            def _(sp):
                for name in names:
                    sp.dma_start(k[name][:], w[name]).then_inc(w_in, 16)
                sp.wait_ge(w_pool, 1)
                for row in (0, PW - 1):
                    sp.dma_start(vpad_d[:, :, row, :].rearrange("b c w -> c b w"), zpad[:]).then_inc(pad_out, 16)
                    for part in range(3):
                        sp.dma_start(cpad_d[:, part * C:(part + 1) * C, row, :].rearrange("b c w -> c b w"),
                                     zpadb[:]).then_inc(pad_out, 16)
                sp.wait_ge(pad_out, 8 * 16)
                for s, start in ahead:
                    sp.sem_inc(s, start)

            @block.gpsimd
            def _(pool):
                pool.memset(zpad[:], 0.0)
                pool.memset(zpadb[:], 0.0).then_inc(w_pool, 1)
                for i in range(2):
                    pool.memset(a_vT[i][:], 0.0)
                    pool.memset(a_v[i][:, :, :, 2 * HD:VH], 1.0)
                pool.memset(c_hmp[:], 0.0)
                pool.memset(c_lop[:], 0.0)

            @block.vector
            def _(dve):
                xTs = a_xT + [cb_[0]["xT"], cb_[1]["xT"]]
                for d in cb_:
                    dve.memset(d["cwT"][:, :], 0.0)
                for xT in xTs:
                    last = dve.memset(xT[C:128, :], 0.0)
                last.then_inc(w_dve, 1)
                dve.wait_ge(w_dve, 1)
                for xT in xTs:
                    dve.memset(xT[C:C + 1, :], 1.0)
                dve.wait_ge(w_in, 16 * len(names))
                alone(dve)
                up, low = slice(0, C), slice(C, 128)
                for n, (half, tap) in enumerate([(up, dx) for dx in range(3)] + [(low, 3 + dx) for dx in range(3)] +
                                                [(up, 6), (low, 7), (up, 8)]):
                    dve.tensor_scalar(out=lepe_tap[half, (0, 1, 2, 0, 1, 2, 3, 3, 4)[n], :], in0=k["outT"][half, :],
                                      scalar1=k["lepe"][half, tap:tap + 1], scalar2=None, op0=ALU.mult)
                dve.tensor_copy(lepe_tap[low, 4, :], k["outeo"][low, :])
                dve.tensor_copy(ident_b[:, :], k["ident"][:, :])
                steps = 1

                def link(ins):
                    nonlocal steps
                    steps += 1
                    ins.then_inc(w_dve, 1)
                    dve.wait_ge(w_dve, steps)

                link(dve.tensor_scalar(out=k["conv"][:, :, :], in0=k["conv"][:, :, :], scalar1=0.0, scalar2=None, op0=ALU.is_ge))
                link(dve.tensor_scalar(out=conv_tap[:, :, :], in0=k["conv"][:, :, :], scalar1=2.0, scalar2=-1.0, op0=ALU.mult, op1=ALU.add))
                dve.tensor_copy(conv_low[up, 0:3, :], conv_tap[up, 0:3, :])
                dve.tensor_copy(conv_low[low, 0:3, :], conv_tap[low, 3:6, :])
                dve.tensor_copy(conv_low[up, 3:6, :], conv_tap[up, 6:9, :])
                for n in (0, 1):
                    b2 = k[f"b2_{n}"]
                    dve.tensor_copy(sel_b[n][:, :, :], k[f"sel_{n}"][:, :, :])
                    link(dve.tensor_copy(b2_b[n][:, 0, :], b2[:, :]))
                    link(dve.tensor_tensor(out=b2_d[n][:, :], in0=b2[:, :], in1=b2_b[n][:, 0, :], op=ALU.subtract))
                    link(dve.tensor_copy(b2_b[n][:, 1, :], b2_d[n][:, :]))
                    link(dve.tensor_tensor(out=b2_b[n][:, 2, :], in0=b2_d[n][:, :], in1=b2_b[n][:, 1, :], op=ALU.subtract))
                dve.wait_ge(w_pe, 1)
                dve.tensor_tensor(out=out_bias[:, :], in0=a_ps[0:C, 0:1], in1=k["outb"][:, :], op=ALU.add)

            @block.tensor
            def _(pe):
                pe.wait_ge(w_in, 16 * len(names))
                alone(pe)
                pe.matmul(a_ps[0:C, 0:1], k["outT"][0:C, :], k["lepeb"][:, :], start=True, stop=True).then_inc(w_pe, 1)

        with nc.Block() as block:
            @block.sync
            def _(sp):
                def turn(n, lo):
                    b, first, last = n - B_TURNS[0], lo == B_TURNS[0], lo == B_TURNS[1] - 1
                    on = B_TURNS[0] <= lo < B_TURNS[1]
                    if first:
                        for r in range(AHEAD):
                            sp_gather(sp, b, r)
                    for r in range(SLOTS):
                        if on:
                            if r + AHEAD < SLOTS or not last:
                                sp_gather(sp, b, r + AHEAD)
                            if r == 3 and not first:
                                sp_strip(sp, b - 1, 1)
                            if r == NWIN + 3:
                                sp_strip(sp, b, 0)
                        elif lo == B_TURNS[1] and r == 3:
                            sp_strip(sp, b - 1, 1)
                        steps(sp, "sp", n, lo, r, dict(a=sp_a, t=sp_t, c=sp_c), 0, 1)
                run(sp, turn)
                sp.wait_ge(cs[1]["out"], 16 * NSTRIP + 16)
                alone(sp)
                sp.wait_ge(cs[0]["out"], 16 * NSTRIP + 16)
                alone(sp)
                sp.wait_ge(cs[0]["pout"], 32 * NSTRIP + 32)
                alone(sp)
                for i in range(2):
                    sp.wait_ge(t_out[i], 16 * TURNS + 16)
                    alone(sp)
                    sp.wait_ge(b_out[i], 16 * TURNS + 16)
                    alone(sp)

            @block.tensor
            def _(pe):
                fs = dict(a=pe_a, t=pe_t, c=pe_c)

                def turn(n, lo):
                    b, first, last = n - B_TURNS[0], lo == B_TURNS[0], lo == B_TURNS[1] - 1
                    on = B_TURNS[0] <= lo < B_TURNS[1]
                    if first:
                        pe_scores(pe, b, 0)
                        pe_scores(pe, b, 1)
                    for r in range(SLOTS):
                        before = on and (r >= 1 or not first)
                        steps(pe, "pe", n, lo, r, fs, 0, 0.2)
                        if before:
                            pe_turn(pe, b, r - 1, 0)
                        if on and (r + 2 < SLOTS or not last):
                            pe_scores(pe, b, r + 2)
                        if before:
                            pe_turn(pe, b, r - 1, 1)
                        steps(pe, "pe", n, lo, r, fs, 0.2, 0.4)
                        if on and (r >= 3 or not first):
                            pe_out(pe, b, r - 3, r - 2)
                        steps(pe, "pe", n, lo, r, fs, 0.4, 0.6)
                        if before:
                            pe_values(pe, b, r - 1)
                        steps(pe, "pe", n, lo, r, fs, 0.6, 1)
                    if last:
                        pe_out(pe, b, SLOTS - 3, SLOTS - 2)
                        pe_turn(pe, b, SLOTS - 1, 0)
                        pe_turn(pe, b, SLOTS - 1, 1)
                        pe_values(pe, b, SLOTS - 1)
                        pe_out(pe, b, SLOTS - 2, SLOTS - 1)
                        pe_out(pe, b, SLOTS - 1, SLOTS - 1)
                run(pe, turn)

            @block.scalar
            def _(act):
                fs = dict(a=act_a, t=act_t, c=act_c)

                def turn(n, lo):
                    b, first, last = n - B_TURNS[0], lo == B_TURNS[0], lo == B_TURNS[1] - 1
                    on = B_TURNS[0] <= lo < B_TURNS[1]
                    if first:
                        act_scores(act, b, 0)
                        act_scores(act, b, 1)
                    for r in range(SLOTS):
                        before = on and (r >= 1 or not first)
                        if on:
                            act_exp(act, b, r)
                        steps(act, "act", n, lo, r, fs, 0, 0.2)
                        if before:
                            act_turn(act, b, r - 1, 0)
                        if on and (r + 2 < SLOTS or not last):
                            act_scores(act, b, r + 2)
                        if before:
                            act_turn(act, b, r - 1, 1)
                        steps(act, "act", n, lo, r, fs, 0.2, 0.4)
                        if on and (r >= 3 or not first):
                            act_out(act, b, r - 3)
                        steps(act, "act", n, lo, r, fs, 0.4, 0.6)
                        if before:
                            act_values(act, b, r - 1)
                        steps(act, "act", n, lo, r, fs, 0.6, 1)
                    if last:
                        act_out(act, b, SLOTS - 3)
                        act_turn(act, b, SLOTS - 1, 0)
                        act_turn(act, b, SLOTS - 1, 1)
                        act_values(act, b, SLOTS - 1)
                        act_out(act, b, SLOTS - 2)
                        act_out(act, b, SLOTS - 1)
                run(act, turn)

            @block.vector
            def _(dve):
                def turn(n, lo):
                    b, first, last = n - B_TURNS[0], lo == B_TURNS[0], lo == B_TURNS[1] - 1
                    on = B_TURNS[0] <= lo < B_TURNS[1]
                    for r in range(SLOTS):
                        if on:
                            dve_select(dve, b, r, r - 3 if r >= 3 or not first else None)
                            if r >= 3 or not first:
                                dve_norm(dve, b, r - 3)
                        steps(dve, "dve", n, lo, r, dict(a=dve_a, t=dve_t, c=dve_c), 0, 1)
                    if last:
                        for r in range(SLOTS - 3, SLOTS):
                            dve_recip(dve, b, r)
                            dve_norm(dve, b, r)
                run(dve, turn)

            @block.gpsimd
            def _(pool):
                fs = dict(a=pool_a, c=pool_c)

                def turn(n, lo):
                    b, first, last = n - B_TURNS[0], lo == B_TURNS[0], lo == B_TURNS[1] - 1
                    on = B_TURNS[0] <= lo < B_TURNS[1]
                    if first:
                        for r in range(3):
                            pool_spread(pool, b, r)
                    for r in range(SLOTS):
                        if on:
                            pool_mask(pool, b, r)
                        steps(pool, "pool", n, lo, r, fs, 0.2, 0.3)
                        if on and (r + 3 < SLOTS or not last):
                            pool_spread(pool, b, r + 3)
                        steps(pool, "pool", n, lo, r, fs, 0.3, 0.5)
                        if on:
                            pool_prob(pool, b, r)
                        steps(pool, "pool", n, lo, r, fs, 0.5, 1)
                run(pool, turn)


def kernel(**inputs):
    import numpy as np
    import concourse.bacc as bacc
    from concourse.bass_utils import run_bass_kernel_spmd as run

    a = {n: np.asarray(v) for n, v in inputs.items()}
    f = np.float32
    lay = {}

    def full(v):
        return np.concatenate([v, np.zeros((128 - len(v),) + v.shape[1:], f)])

    lay["wqkv"] = full(np.concatenate([a["L0_conv_qkv_w"].T, a["L0_conv_qkv_b"][None, :]]))
    lay["outT"] = np.tile(a["L0_conv_out_w"].T, (2, 1))
    lay["outeo"] = np.tile(a["L0_conv_out_w"].T.reshape(HP, 2, HD, C).transpose(1, 0, 2, 3).reshape(C, C), (2, 1))
    lay["outb"] = a["L0_conv_out_b"].reshape(C, 1)
    lay["lepe"] = np.tile(a["L0_conv_lepe_w"].reshape(C, 9), (2, 1))
    lay["lepeb"] = a["L0_conv_lepe_b"].reshape(C, 1)
    lay["conv"] = np.tile(a["L1_conv_kernel"].reshape(9, C, C).transpose(1, 0, 2), (2, 1, 1))
    lay["gate_0"] = full(np.concatenate([a["L0_ffn_router_w"].T, np.zeros((1, NE), f)]))
    lay["gate_1"] = full(np.concatenate([a["L1_ffn_gate_w"], a["L1_ffn_gate_b"][None, :]]))
    lay["w1_0"] = full(a["L0_ffn_w1"].reshape(4, 2, C, C).transpose(2, 0, 1, 3).reshape(C, 4, 128))
    lay["b1_0"] = a["L0_ffn_b1"].reshape(4, 128).T
    lay["w2_0"] = a["L0_ffn_w2"].reshape(4, 128, C).transpose(1, 0, 2)
    lay["b2_0"] = full(np.tile(a["L0_ffn_b2"], (3, 1)))
    lay["w1_1"] = full(a["L1_ffn_W1"].transpose(1, 0, 2))
    lay["b1_1"] = a["L1_ffn_b1"].T
    lay["w2_1"] = a["L1_ffn_W2"].transpose(1, 0, 2)
    lay["b2_1"] = full(np.tile(a["L1_ffn_b2"], (3, 1)))
    rows = np.arange(128)
    lay["ident"] = np.eye(128, dtype=f)
    lay["head"] = ((rows // HD)[:, None] == np.arange(2 * NHEAD)[None, :]).astype(f) * f(C ** -0.5)
    expert = np.arange(NE)
    expert3 = np.arange(3 * NE) % NE
    lay["sel_0"] = full((expert3[:, None, None] == 2 * np.arange(4)[None, :, None] + (rows // C)[None, None, :]).astype(f))
    lay["sel_1"] = full(np.broadcast_to((expert3[:, None, None] == expert[None, :, None]), (3 * NE, NE, 128)).astype(f))
    lay["iota"] = np.broadcast_to(expert.astype(f), (128, NE))
    lay["mhalf"] = np.full((128, NT), -0.5, f)

    nc = bacc.Bacc("TRN2", target_bir_lowering=False, num_devices=1)
    arrays = {"in_x": np.ascontiguousarray(a["x"])}
    x = nc.dram_tensor("in_x", a["x"].shape, F32, kind="ExternalInput").ap()
    w = {}
    for name, v in lay.items():
        v = np.ascontiguousarray(v)
        arrays["in_" + name] = v
        w[name] = nc.dram_tensor("in_" + name, v.shape, F32, kind="ExternalInput").ap()
    out = nc.dram_tensor("out_0", (B, H, W, C), F32, kind="ExternalOutput").ap()
    program(nc, x, out, w)
    r = run(nc, [arrays], core_ids=[0])
    return r.results[0]["out_0"]
```
